# Optimizing a Trainium2 kernel written in Bass

```python
import numpy as np
import jax
import jax.numpy as jnp

def _softmax(x, axis=-1):
    return jax.nn.softmax(x, axis=axis)

def _gelu(x):
    return jax.nn.gelu(x, approximate=True)

def _silu(x):
    return jax.nn.silu(x)

def _sigmoid(x):
    return jax.nn.sigmoid(x)

def _layernorm(x, axis=-1, eps=1e-05):
    m = jnp.mean(x, axis=axis, keepdims=True)
    v = jnp.var(x, axis=axis, keepdims=True)
    return (x - m) / jnp.sqrt(v + eps)

def _scatter_add(tgt, idx, src, axis=0):
    return tgt.at[idx].add(src)

def _segment_sum(src, seg, n):
    return jax.ops.segment_sum(src, seg, n)
kernel_name = 'mk_perceiver_d1_seqx_r2_0fbcc1'

def setup_inputs(seed: int=0):
    np.random.seed(seed)
    _w = jnp.asarray

    def _rec_inputs():
        import jax
        import jax.numpy as jnp
        _rk = jax.random.key(seed)
        x = 0.0002417 + 0.9998 * jax.random.normal(jax.random.fold_in(_rk, 1), (1, 256, 512), jnp.float32)
        _lenS = 256 - jax.random.randint(jax.random.fold_in(_rk, 7), (1,), 0, max(1, 256 // 4) + 1, jnp.int32)
        _lenS2 = 25088 - jax.random.randint(jax.random.fold_in(_rk, 8), (1,), 0, max(1, 25088 // 4) + 1, jnp.int32)
        _ctx_1024P = jax.random.normal(jax.random.fold_in(_rk, 11), (1, 16, 512), jnp.float32)
        _ctx_1024c = jax.random.dirichlet(jax.random.fold_in(_rk, 511), 0.3 * jnp.ones((16,), jnp.float32), (1, 25088))
        _ctx_1024t = jnp.einsum('bsk,bkd->bsd', _ctx_1024c, _ctx_1024P)
        _ctx_1024t = _ctx_1024t * jax.lax.rsqrt(jnp.mean(jnp.square(_ctx_1024t)) + 1e-12) * 0.953939
        ctx_1024 = 7.22013e-05 + 1.00017 * (_ctx_1024t + 0.3 * jax.random.normal(jax.random.fold_in(_rk, 611), (1, 25088, 512), jnp.float32))
        return (x, ctx_1024)
    x, ctx_1024 = _rec_inputs()

    def _L0_xattn_setup():
        import jax, jax.numpy as jnp
        import numpy as np
        D_MODEL = 512
        B, S = (4, 1024)
        key = jax.random.key(seed)
        ks = jax.random.split(key, 10)
        s = 1.0 / np.sqrt(D_MODEL)
        return {'k': jax.random.normal(ks[0], (B, S, D_MODEL), jnp.float32), 'v': jax.random.normal(ks[1], (B, S, D_MODEL), jnp.float32), 'q': jax.random.normal(ks[2], (B, S, D_MODEL), jnp.float32), 'Wk': jax.random.normal(ks[3], (D_MODEL, D_MODEL), jnp.float32) * s, 'Wv': jax.random.normal(ks[4], (D_MODEL, D_MODEL), jnp.float32) * s, 'bv': jnp.zeros((D_MODEL,), jnp.float32), 'Wq': jax.random.normal(ks[5], (D_MODEL, D_MODEL), jnp.float32) * s, 'bq': jnp.zeros((D_MODEL,), jnp.float32), 'Wo': jax.random.normal(ks[6], (D_MODEL, D_MODEL), jnp.float32) * s, 'bo': jnp.zeros((D_MODEL,), jnp.float32)}
    _L0_xattn_all = _L0_xattn_setup()
    _L0_xattn_in = {k: v for k, v in _L0_xattn_all.items() if k in ('Wk', 'Wv', 'bv', 'Wq', 'bq', 'Wo', 'bo')}
    del _L0_xattn_all

    def _L0_attn_setup():
        import jax, jax.numpy as jnp
        import numpy as np
        B, N, D, OUT = (8, 1024, 512, 512)
        MEM = 21

        def _xavier(key, shape):
            fan_in, fan_out = (shape[0], shape[1])
            lim = (6.0 / (fan_in + fan_out)) ** 0.5
            return jax.random.uniform(key, shape, jnp.float32, -lim, lim)
        key = jax.random.key(seed)
        k1, k2, k3, k4, k5 = jax.random.split(key, 5)
        input_data = jax.random.normal(k1, (B, N, D), jnp.float32)
        W1 = _xavier(k2, (D, OUT))
        W2 = _xavier(k3, (D, OUT))
        bias = jax.random.normal(k4, (OUT,), jnp.float32)
        table = _xavier(k5, (MEM, D))
        table = table.at[0].set(0.0)
        return {'input_data': input_data, 'W1': W1, 'W2': W2, 'bias': bias, 'embeddings_table': table}
    _L0_attn_all = _L0_attn_setup()
    _L0_attn_in = {k: v for k, v in _L0_attn_all.items() if k in ('W1', 'W2', 'bias', 'embeddings_table')}
    del _L0_attn_all

    def _L0_ffn_setup():
        import jax, jax.numpy as jnp
        import numpy as np
        B, S, DIM = (2, 1024, 512)
        HID = 1024
        E, NSH, TOPK = (8, 2, 2)

        def _ffn(x, w1, w2, w3):
            return jax.nn.silu(x @ w1.T) * (x @ w3.T) @ w2.T
        key = jax.random.key(seed)
        ks = jax.random.split(key, 8)
        sc = 0.02
        return {'x': jax.random.normal(ks[0], (B, S, DIM), jnp.float32), 'router_w': jax.random.normal(ks[1], (E, DIM), jnp.float32) * sc, 'expert_bias': jnp.zeros((E,), jnp.float32), 'w1': jax.random.normal(ks[2], (E, HID, DIM), jnp.float32) * sc, 'w3': jax.random.normal(ks[3], (E, HID, DIM), jnp.float32) * sc, 'w2': jax.random.normal(ks[4], (E, DIM, HID), jnp.float32) * sc, 'sw1': jax.random.normal(ks[5], (NSH, HID, DIM), jnp.float32) * sc, 'sw3': jax.random.normal(ks[6], (NSH, HID, DIM), jnp.float32) * sc, 'sw2': jax.random.normal(ks[7], (NSH, DIM, HID), jnp.float32) * sc}
    _L0_ffn_all = _L0_ffn_setup()
    _L0_ffn_in = {k: v for k, v in _L0_ffn_all.items() if k in ('router_w', 'expert_bias', 'w1', 'w3', 'w2', 'sw1', 'sw3', 'sw2')}
    del _L0_ffn_all
    return {'x': x, 'ctx_1024': ctx_1024, 'L0_xattn_Wk': _L0_xattn_in['Wk'], 'L0_xattn_Wv': _L0_xattn_in['Wv'], 'L0_xattn_bv': _L0_xattn_in['bv'], 'L0_xattn_Wq': _L0_xattn_in['Wq'], 'L0_xattn_bq': _L0_xattn_in['bq'], 'L0_xattn_Wo': _L0_xattn_in['Wo'], 'L0_xattn_bo': _L0_xattn_in['bo'], 'L0_attn_W1': _L0_attn_in['W1'], 'L0_attn_W2': _L0_attn_in['W2'], 'L0_attn_bias': _L0_attn_in['bias'], 'L0_attn_embeddings_table': _L0_attn_in['embeddings_table'], 'L0_ffn_router_w': _L0_ffn_in['router_w'], 'L0_ffn_expert_bias': _L0_ffn_in['expert_bias'], 'L0_ffn_w1': _L0_ffn_in['w1'], 'L0_ffn_w3': _L0_ffn_in['w3'], 'L0_ffn_w2': _L0_ffn_in['w2'], 'L0_ffn_sw1': _L0_ffn_in['sw1'], 'L0_ffn_sw3': _L0_ffn_in['sw3'], 'L0_ffn_sw2': _L0_ffn_in['sw2']}

def reference(x, ctx_1024, L0_xattn_Wk, L0_xattn_Wv, L0_xattn_bv, L0_xattn_Wq, L0_xattn_bq, L0_xattn_Wo, L0_xattn_bo, L0_attn_W1, L0_attn_W2, L0_attn_bias, L0_attn_embeddings_table, L0_ffn_router_w, L0_ffn_expert_bias, L0_ffn_w1, L0_ffn_w3, L0_ffn_w2, L0_ffn_sw1, L0_ffn_sw3, L0_ffn_sw2):
    import jax
    import jax.numpy as jnp

    def _L0_xattn_ref(k, v, q, Wk, Wv, bv, Wq, bq, Wo, bo):
        import jax, jax.numpy as jnp
        import numpy as np
        D_MODEL = 512
        B, S = (4, 1024)
        kp = jnp.einsum('bsd,ed->bse', k, Wk)
        vp = jnp.einsum('bsd,ed->bse', v, Wv) + bv
        qp = jnp.einsum('bsd,ed->bse', q, Wq) + bq
        scale = 1.0 / jnp.sqrt(jnp.float32(kp.shape[-1]))
        scores = jnp.einsum('bqd,bkd->bqk', qp, kp) * scale
        probs = jax.nn.softmax(scores, axis=-1)
        ctx = jnp.einsum('bqk,bkd->bqd', probs, vp)
        return jnp.einsum('bqd,ed->bqe', ctx, Wo) + bo

    def _L0_attn_ref(input_data, W1, W2, bias, embeddings_table):
        import jax, jax.numpy as jnp
        import numpy as np
        B, N, D, OUT = (8, 1024, 512, 512)
        MEM = 21

        def _xavier(key, shape):
            fan_in, fan_out = (shape[0], shape[1])
            lim = (6.0 / (fan_in + fan_out)) ** 0.5
            return jax.random.uniform(key, shape, jnp.float32, -lim, lim)
        Bn, Nn, Dn = input_data.shape
        M = embeddings_table.shape[0]
        et = embeddings_table.at[0].set(0.0)
        x_c = jnp.transpose(input_data, (0, 2, 1))
        w = jnp.transpose(et)[:, None, ::-1]
        h_hatt = jax.lax.conv_general_dilated(x_c, w, window_strides=(1,), padding=[(M - 1, 0)], dimension_numbers=('NCH', 'OIH', 'NCH'), feature_group_count=Dn)
        h_hatt = jnp.transpose(h_hatt, (0, 2, 1))
        return input_data @ W1 + h_hatt @ W2 + bias

    def _L0_ffn_ref(x, router_w, expert_bias, w1, w3, w2, sw1, sw3, sw2):
        import jax, jax.numpy as jnp
        import numpy as np
        B, S, DIM = (2, 1024, 512)
        HID = 1024
        E, NSH, TOPK = (8, 2, 2)

        def _ffn(x, w1, w2, w3):
            return jax.nn.silu(x @ w1.T) * (x @ w3.T) @ w2.T
        bs, sl, d = x.shape
        xf = x.reshape(-1, d)
        shared = jnp.zeros_like(xf)
        for i in range(sw1.shape[0]):
            shared = shared + _ffn(xf, sw1[i], sw2[i], sw3[i])
        logits = xf @ router_w.T + expert_bias
        rw, sel = jax.lax.top_k(logits, TOPK)
        rw = jax.nn.softmax(rw.astype(jnp.float32), axis=-1).astype(x.dtype)
        onehot = jax.nn.one_hot(sel, E, dtype=x.dtype)
        combine = jnp.einsum('tk,tke->te', rw, onehot)

        def body(acc, ew):
            e1, e3, e2, cw = ew
            acc = acc + cw[:, None] * _ffn(xf, e1, e2, e3)
            return (acc, None)
        out, _ = jax.lax.scan(body, jnp.zeros_like(xf), (w1, w3, w2, combine.T))
        out = out + shared
        return out.reshape(bs, sl, -1)
    x = x + _L0_xattn_ref(ctx_1024, ctx_1024, _layernorm(x, axis=-1), L0_xattn_Wk, L0_xattn_Wv, L0_xattn_bv, L0_xattn_Wq, L0_xattn_bq, L0_xattn_Wo, L0_xattn_bo)
    x = x + _L0_attn_ref(_layernorm(x, axis=-1), L0_attn_W1, L0_attn_W2, L0_attn_bias, L0_attn_embeddings_table)
    x = x + _L0_ffn_ref(_layernorm(x, axis=-1), L0_ffn_router_w, L0_ffn_expert_bias, L0_ffn_w1, L0_ffn_w3, L0_ffn_w2, L0_ffn_sw1, L0_ffn_sw3, L0_ffn_sw2)
    return x

_drawn_inputs = setup_inputs


def setup_inputs(seed=0):
    import zlib

    import numpy as np

    out = dict(_drawn_inputs(seed))
    spreads = {'L0_xattn_bv': (0.0, 0.1),
     'L0_xattn_bq': (0.0, 0.409),
     'L0_xattn_bo': (0.0, 0.1),
     'L0_ffn_expert_bias': (0.0, 2.0)}
    factors = {'L0_ffn_router_w': 4.091}
    for name, (base, spread) in spreads.items():
        noise = np.random.default_rng([zlib.crc32(name.encode()), seed]).standard_normal(out[name].shape)
        drawn = base * np.exp(spread * noise) if base else spread * noise
        out[name] = jnp.asarray(drawn.astype(out[name].dtype))
    for name, factor in factors.items():
        out[name] = (out[name] * factor).astype(out[name].dtype)
    return out
```

```python
from contextlib import ExitStack
import math

import concourse.bass as bass
from concourse import mybir

P = 128
F32 = mybir.dt.float32
F16 = mybir.dt.float16
U32 = mybir.dt.uint32
ALU = mybir.AluOpType
ACT = mybir.ActivationFunctionType
AX = mybir.AxisListType

D = 512
DC = D // P
TOK = 256
TB = TOK // P
KEYS = 25088
KT = 7
GK = KT * P
NG = KEYS // GK
HALF = GK // 2
PAIRS = 4
TAPS = 21
NE = 8
NS = 2
NX = NS + NE
HID = 1024
HB = HID // P
PIECE = 2048
PIECES = 3 * 4096 // PIECE
RAW = 3
SC = 1.0 / math.sqrt(D)
LN_P = 12 * math.log(2.0)
WSC = 64.0
EPS = 1e-5


def need(eng, sem, count):
    if not (isinstance(count, int) and count <= 0):
        eng.wait_ge(sem, count)


def perceiver_kernel(nc, x, ctx_nat, ctx_t, wmats, bq, bv, bo, bias, table, router, ebias, wexp, out):
    with ExitStack() as keep:
        def sb(name, shape, dt, stack=keep):
            return stack.enter_context(nc.sbuf_tensor(name, shape, dt))

        def sem(name):
            return keep.enter_context(nc.semaphore(name))

        ident = sb("ident", [P, P], F32)
        x_sb = sb("x_sb", [P, TB, D], F32)
        x1 = sb("x1", [P, TB, D], F32)
        acc = sb("acc", [P, TB, D], F32)
        wts = sb("wts", [P, 4, DC, D], F32)
        bo_b = sb("bo_b", [P, D], F32)
        bias_b = sb("bias_b", [P, D], F32)
        ebias_b = sb("ebias_b", [P, NE], F32)
        bq_sb = sb("bq_sb", [P, DC], F32)
        bv_sb = sb("bv_sb", [P, DC], F32)
        table_sb = sb("table_sb", [P, DC, TAPS], F32)
        router_sb = sb("router_sb", [P, DC, NE], F32)
        stats = sb("stats", [P, TB, 6], F32)
        mv = sb("mv", [P, TB, 2], F32)
        var_e = sb("var_e", [P, TB], F32)
        std = sb("std", [P, TB], F32)
        rstd = sb("rstd", [P, TB], F32)
        mx = sb("mx", [P, 2, TB], F32)
        cm = sb("cm", [P, TB], F32)
        nb = sb("nb", [P, 2, TB], F32)
        dm = sb("dm", [P, 2, TB], F32)
        alpha = sb("alpha", [P, 2, TB], F32)
        rs = sb("rs", [P, 2, TB], F32)
        den = sb("den", [P, TB], F32)
        rden = sb("rden", [P, TB], F32)
        iota8 = sb("iota8", [P, NE], F32)
        logits = sb("logits", [P, TB, NE], F32)
        top = sb("top", [P, TB, 8], F32)
        topi = sb("topi", [P, TB, 8], U32)
        topf = sb("topf", [P, TB, 8], F32)
        pr = sb("pr", [P, TB, 4], F32)
        sel = sb("sel", [P, TB, 2, NE], F32)
        comb = sb("comb", [P, TB, NX], F32)

        att = ExitStack()
        rawT = sb("rawT", [P, 2, DC, GK], F32, att)
        rawN = sb("rawN", [P, 2, KT, D], F32, att)
        cTh = sb("cTh", [P, 2, DC, GK], F16, att)
        cTl = sb("cTl", [P, 2, DC, GK], F16, att)
        cNh = sb("cNh", [P, 2, KT, D], F16, att)
        cNl = sb("cNl", [P, 2, KT, D], F16, att)
        prob = sb("prob", [P, TB, GK], F32, att)
        pTh = sb("pTh", [P, KT, TOK], F16, att)
        pTl = sb("pTl", [P, KT, TOK], F16, att)
        qTh = sb("qTh", [P, DC, TOK], F16, att)
        qTl = sb("qTl", [P, DC, TOK], F16, att)
        att.close()
        wraw = sb("wraw", [P, RAW, PIECE], F32)
        wh = sb("wh", [P, 2, PIECES, PIECE], F16)
        wl = sb("wl", [P, 2, PIECES, PIECE], F16)
        t1 = sb("t1", [P, DC, TOK], F32)
        t2 = sb("t2", [P, DC, TOK], F32)
        xpad = sb("xpad", [P, DC, TAPS - 1 + TOK], F32)
        macc = sb("macc", [P, TB, D], F32)
        xTh = sb("xTh", [P, DC, TOK], F16)
        xTl = sb("xTl", [P, DC, TOK], F16)
        sil = sb("sil", [P, 2, TOK], F32)
        hf = sb("hf", [P, 2, TOK], F32)
        hh = sb("hh", [P, 4, TOK], F16)
        hl = sb("hl", [P, 4, TOK], F16)

        xn = prob[:, :, 0:D]
        xnT = rawN[:, 1, 0:2, :].rearrange("p a (b t) -> p (a b) t", t=TOK)
        qpT = rawN[:, 1, 2:4, :].rearrange("p a (b t) -> p (a b) t", t=TOK)

        ps = keep.enter_context(nc.psum_tensor("ps", [P, 8, 512], F32))
        psS = ps[:, 0:4, :]
        psT = ps[:, 4:6, :]
        psO = ps[:, 6:8, :]

        def cols(bank):
            return ps[:, bank:bank + 2, :].rearrange("p a (b t) -> p (a b) t", t=TOK)

        def w13(t, par, m):
            return t[:, par, 2 * m:2 * m + 2, :].rearrange("p a (c h) -> p (a c) h", h=HID)

        def w2(t, par):
            return t[:, par, 4:6, :].rearrange("p a (c n) -> p (a c) n", n=D)

        s_x = sem("s_x")
        s_wqk = sem("s_wqk")
        s_small = sem("s_small")
        s_wvo = sem("s_wvo")
        s_w12 = sem("s_w12")
        s_rawT = [sem(f"s_rawT{i}") for i in range(2)]
        s_rawN = [sem(f"s_rawN{i}") for i in range(2)]
        s_ident = sem("s_ident")
        s_iota = sem("s_iota")
        s_init = sem("s_init")
        s_ln = sem("s_ln")
        s_std = sem("s_std")
        s_pe = sem("s_pe")
        s_ev = sem("s_ev")
        s_qh = sem("s_qh")
        s_ql = sem("s_ql")
        s_hiT = sem("s_hiT")
        s_loT = sem("s_loT")
        s_hiN = sem("s_hiN")
        s_loN = sem("s_loN")
        s_S = sem("s_S")
        s_cm = sem("s_cm")
        s_mx = sem("s_mx")
        s_ref = sem("s_ref")
        s_alpha = sem("s_alpha")
        s_exp = sem("s_exp")
        s_T = sem("s_T")
        s_pth = sem("s_pth")
        s_ptl = sem("s_ptl")
        s_PV = sem("s_PV")
        s_acc = sem("s_acc")
        s_den = sem("s_den")
        s_mid = sem("s_mid")
        s_zt = sem("s_zt")
        s_zero = sem("s_zero")
        s_gap = sem("s_gap")
        s_wraw = [sem(f"s_wraw{i}") for i in range(RAW)]
        s_whi = sem("s_whi")
        s_wlo = sem("s_wlo")
        s_H = sem("s_H")
        s_sil = sem("s_sil")
        s_h = sem("s_h")
        s_hh = sem("s_hh")
        s_hl = sem("s_hl")
        s_h2 = sem("s_h2")
        s_Y = sem("s_Y")
        s_macc = sem("s_macc")
        s_out = sem("s_out")

        PAIR_TILES = [(0, 2), (2, 4), (4, 6), (6, 7)]
        tok_view = lambda a: a.rearrange("o (b p) d -> p (o b) d", p=P)

        block = keep.enter_context(nc.Block())

        @block.sync
        def _(sp):
            sp.dma_start(x_sb[:], tok_view(x)).then_inc(s_x, 16)
            for m in range(2):
                sp.dma_start(wts[:, m], wmats[m]).then_inc(s_wqk, 16)
            small = [(bq_sb[:], bq), (bv_sb[:], bv), (table_sb[:], table), (router_sb[:], router),
                     (bo_b[:], bo.partition_broadcast(P)), (bias_b[:], bias.partition_broadcast(P)),
                     (ebias_b[:], ebias.partition_broadcast(P))]
            for dst, src in small:
                sp.dma_start(dst, src).then_inc(s_small, 16)

            def load_t(g, slot):
                sp.dma_start(rawT[:, slot], ctx_t[g]).then_inc(s_rawT[slot], 16)

            def load_n(g, slot):
                sp.dma_start(rawN[:, slot], ctx_nat[g]).then_inc(s_rawN[slot], 16)

            def split_t(count):
                sp.wait_ge(s_hiT, 4 * count)
                sp.wait_ge(s_loT, 4 * count)

            def split_n(count):
                sp.wait_ge(s_hiN, 4 * count)
                sp.wait_ge(s_loN, 4 * count)

            load_t(0, 0)
            load_n(0, 0)
            load_t(1, 1)
            split_t(1)
            load_t(2, 0)
            sp.wait_ge(s_qh, 1)
            sp.wait_ge(s_ql, 1)
            load_n(1, 1)
            split_t(2)
            load_t(3, 1)
            split_n(1)
            load_n(2, 0)
            for m in range(2):
                sp.dma_start(wts[:, m], wmats[2 + m]).then_inc(s_wvo, 16)
            for m in range(2):
                sp.dma_start(wts[:, 2 + m], wmats[4 + m]).then_inc(s_w12, 16)
            with sp.Fori(2, NG // 2) as i:
                split_t(2 * i - 1)
                load_t(2 * i, 0)
                split_n(2 * i - 2)
                load_n(2 * i - 1, 1)
                split_t(2 * i)
                load_t(2 * i + 1, 1)
                split_n(2 * i - 1)
                load_n(2 * i, 0)
            split_n(NG - 2)
            load_n(NG - 1, 1)

            def load_piece(e, k):
                sp.dma_start(wraw[:, k % RAW], wexp[e, :, k * PIECE:(k + 1) * PIECE]).then_inc(s_wraw[k % RAW], 16)

            split_t(NG)
            for k in range(RAW):
                load_piece(0, k)
            for k in range(RAW, PIECES):
                sp.wait_ge(s_wlo, k - RAW + 1)
                load_piece(0, k)
            with sp.Fori(1, NX) as e:
                for k in range(PIECES):
                    sp.wait_ge(s_wlo, PIECES * e + k - RAW + 1)
                    load_piece(e, k)
            for b in range(TB):
                sp.wait_ge(s_macc, TB * NX - TB + b + 1)
                sp.dma_start(tok_view(out)[:, b, :], macc[:, b, :]).then_inc(s_out, 16)
            sp.wait_ge(s_out, 16 * TB)

        @block.gpsimd
        def _(pool):
            nc.gpsimd.memset(ident[:], 0.0).then_inc(s_ident, 1)
            pool.wait_ge(s_ident, 1)
            nc.gpsimd.affine_select(out=ident[:], in_=ident[:], compare_op=ALU.not_equal, fill=1.0, base=0,
                                    pattern=[[-1, P]], channel_multiplier=1).then_inc(s_ident, 1)
            nc.gpsimd.iota(iota8[:], pattern=[[1, NE]], base=0, channel_multiplier=0,
                           allow_small_or_imprecise_dtypes=True).then_inc(s_iota, 1)
            nc.gpsimd.memset(comb[:, :, 0:NS], 1.0 / (WSC * WSC)).then_inc(s_iota, 1)

        @block.scalar
        def _(act):
            def root(n):
                act.wait_ge(s_ln, 6 * n + 4)
                nc.scalar.activation(std[:], var_e[:], ACT.Sqrt).then_inc(s_std, 1)

            def hi_t(g, par, c):
                nc.scalar.activation(cTh[:, par, c], rawT[:, par, c], ACT.Copy).then_inc(s_hiT, 1)

            def hi_n(par, j):
                a, b = PAIR_TILES[j]
                nc.scalar.activation(cNh[:, par, a:b], rawN[:, par, a:b], ACT.Copy).then_inc(s_hiN, 1)

            def landed(sems, g, par):
                act.wait_ge(sems[par], (g - par) * 8 + 16)

            def softmax(n, par):
                act.wait_ge(s_ref, 2 * n + 2)
                need(act, s_acc, 2 * n - 2)
                nc.scalar.activation(alpha[:, par, :], dm[:, par, :], ACT.Exp, scale=SC).then_inc(s_alpha, 1)
                need(act, s_T, PAIRS * n)
                for b in range(TB):
                    nc.scalar.activation(prob[:, b].rearrange("p (h k) -> p h k", h=2), psS[:, 2 * b:2 * b + 2, 0:HALF],
                                         ACT.Exp, bias=nb[:, par, b:b + 1], scale=SC,
                                         accum_out=rs[:, par, b:b + 1]).then_inc(s_exp, 1)

            def prob_hi(g, j):
                a, b = PAIR_TILES[j]
                act.wait_ge(s_T, PAIRS * g + j + 1)
                nc.scalar.activation(pTh[:, a:b], psT[:, j % 2, 0:(b - a) * TOK].rearrange("p (a t) -> p a t", t=TOK),
                                     ACT.Copy).then_inc(s_pth, 1)

            root(0)
            landed(s_rawT, 0, 0)
            for c in range(DC):
                hi_t(0, 0, c)
            act.wait_ge(s_pe, 3)
            nc.scalar.activation(qTh[:], cols(4), ACT.Copy).then_inc(s_qh, 1)
            landed(s_rawN, 0, 0)
            for j in range(PAIRS):
                hi_n(0, j)
            landed(s_rawT, 1, 1)
            for c in range(DC):
                hi_t(1, 1, c)
            softmax(0, 0)

            def step(g, par, more_t=True, more=True):
                need(act, s_PV, 2 * g)
                for j in (0, 1):
                    prob_hi(g, j)
                if more_t:
                    landed(s_rawT, g + 2, par)
                    act.wait_ge(s_S, 2 * g + 2)
                    for c in range(DC):
                        hi_t(g + 2, par, c)
                for j in (2, 3):
                    prob_hi(g, j)
                if more:
                    landed(s_rawN, g + 1, 1 - par)
                    for j in (0, 1):
                        hi_n(1 - par, j)
                    softmax(g + 1, 1 - par)
                    for j in (2, 3):
                        hi_n(1 - par, j)

            step(0, 0)
            with act.Fori(0, (NG - 4) // 2) as i:
                step(2 * i + 1, 1)
                step(2 * i + 2, 0)
            step(NG - 3, 1)
            step(NG - 2, 0, more_t=False)
            step(NG - 1, 1, more_t=False, more=False)

            def split_hi(e, par, k):
                act.wait_ge(s_wraw[k % RAW], 32 * e + 16 * (k // RAW) + 16)
                nc.scalar.activation(wh[:, par, k], wraw[:, k % RAW], ACT.Copy, scale=WSC).then_inc(s_whi, 1)

            act.wait_ge(s_PV, 2 * NG)
            for k in range(4):
                split_hi(0, 0, k)
            act.wait_ge(s_pe, 5)
            for c in range(DC):
                nc.scalar.activation(t2[:, c], cols(2)[:, c], ACT.Identity, bias=bv_sb[:, c:c + 1]).then_inc(s_zt, 1)
            root(1)
            for k in range(4, PIECES):
                split_hi(0, 0, k)
            root(2)
            act.wait_ge(s_pe, 10)
            nc.scalar.activation(xTh[:], cols(0), ACT.Copy).then_inc(s_qh, 1)
            act.wait_ge(s_gap, 1)
            nc.scalar.activation(pr[:, :, 1:2], pr[:, :, 0:1], ACT.Exp).then_inc(s_std, 1)

            def silu(i, slot):
                act.wait_ge(s_H, i + 1)
                need(act, s_h, i - 1)
                nc.scalar.activation(sil[:, slot % 2], ps[:, slot, 0:TOK], ACT.Silu, scale=1.0 / WSC).then_inc(s_sil, 1)

            def hidden_hi(i, slot):
                act.wait_ge(s_h, i + 1)
                need(act, s_h2, i - 3)
                nc.scalar.activation(hh[:, slot], hf[:, slot % 2], ACT.Copy).then_inc(s_hh, 1)

            def expert(e, par, more=True):
                for b in range(HB):
                    i = HB * e + b
                    silu(i, b % 4)
                    if more and b >= 2:
                        if b == 2:
                            need(act, s_h2, HB * e)
                        split_hi(e + 1, 1 - par, b - 2)
                    hidden_hi(i, b % 4)

            expert(0, 0)
            with act.Fori(0, (NX - 2) // 2) as i:
                expert(2 * i + 1, 1)
                expert(2 * i + 2, 0)
            expert(NX - 1, 1, more=False)

        @block.vector
        def _(dve):
            V = nc.vector

            def norm(n, src, dst):
                for b in range(TB):
                    V.bn_stats(stats[:, b], src[:, b]).then_inc(s_ln, 1)
                dve.wait_ge(s_ln, 6 * n + 2)
                for b in range(TB):
                    last = V.bn_aggr(mv[:, b], stats[:, b])
                last.then_inc(s_ln, 1)
                dve.wait_ge(s_ln, 6 * n + 3)
                V.tensor_scalar(var_e[:], mv[:, :, 1], EPS, None, ALU.add).then_inc(s_ln, 1)
                dve.wait_ge(s_std, n + 1)
                V.reciprocal(rstd[:], std[:]).then_inc(s_ln, 1)
                dve.wait_ge(s_ln, 6 * n + 5)
                for b in range(TB):
                    last = V.tensor_scalar(dst[:, b], src[:, b], mv[:, b, 0:1], rstd[:, b:b + 1],
                                           ALU.subtract, ALU.mult)
                last.then_inc(s_ln, 1)

            def lo_t(g, par, c):
                dve.wait_ge(s_hiT, 4 * g + c + 1)
                V.tensor_tensor(cTl[:, par, c], rawT[:, par, c], cTh[:, par, c], ALU.subtract).then_inc(s_loT, 1)

            def lo_n(g, par, j):
                a, b = PAIR_TILES[j]
                dve.wait_ge(s_hiN, 4 * g + j + 1)
                V.tensor_tensor(cNl[:, par, a:b], rawN[:, par, a:b], cNh[:, par, a:b], ALU.subtract).then_inc(s_loN, 1)

            def reference_max(n, par):
                for b in range(TB):
                    dve.wait_ge(s_S, 2 * n + b + 1)
                    V.tensor_reduce(cm[:, b:b + 1], psS[:, 2 * b:2 * b + 2, 0:HALF], AX.XY, ALU.max).then_inc(s_cm, 1)
                dve.wait_ge(s_cm, 2 * n + 2)
                V.tensor_tensor(mx[:, par], mx[:, 1 - par], cm[:], ALU.max).then_inc(s_mx, 1)
                dve.wait_ge(s_mx, n + 1)
                V.tensor_scalar(nb[:, par], mx[:, par], -SC, LN_P, ALU.mult, ALU.add).then_inc(s_ref, 1)
                V.tensor_tensor(dm[:, par], mx[:, 1 - par], mx[:, par], ALU.subtract).then_inc(s_ref, 1)

            def prob_lo(g, j):
                a, b = PAIR_TILES[j]
                dve.wait_ge(s_pth, PAIRS * g + j + 1)
                V.tensor_tensor(pTl[:, a:b], psT[:, j % 2, 0:(b - a) * TOK].rearrange("p (a t) -> p a t", t=TOK),
                                pTh[:, a:b], ALU.subtract).then_inc(s_ptl, 1)

            def accumulate(g, par):
                dve.wait_ge(s_exp, 2 * g + 2)
                need(dve, s_den, 2 * g)
                for b in range(TB):
                    V.scalar_tensor_tensor(den[:, b:b + 1], den[:, b:b + 1], alpha[:, par, b:b + 1],
                                           rs[:, par, b:b + 1], ALU.mult, ALU.add).then_inc(s_den, 1)
                need(dve, s_acc, 2 * g)
                for b in range(TB):
                    dve.wait_ge(s_PV, 2 * g + b + 1)
                    V.scalar_tensor_tensor(acc[:, b], acc[:, b], alpha[:, par, b:b + 1], psO[:, b],
                                           ALU.mult, ALU.add).then_inc(s_acc, 1)

            V.memset(mx[:], -1e30).then_inc(s_init, 1)
            V.memset(den[:], 0.0).then_inc(s_init, 1)
            V.memset(acc[:], 0.0).then_inc(s_init, 1)
            dve.wait_ge(s_x, 16)
            norm(0, x_sb, xn)
            dve.wait_ge(s_pe, 1)
            V.tensor_copy(xnT, cols(4)).then_inc(s_ev, 1)
            dve.wait_ge(s_pe, 2)
            dve.wait_ge(s_small, 16 * 7)
            for c in range(DC):
                last = V.tensor_scalar(qpT[:, c], cols(6)[:, c], bq_sb[:, c:c + 1], None, ALU.add)
            last.then_inc(s_ev, 1)
            for c in range(DC):
                lo_t(0, 0, c)
            for b in range(TB):
                last = V.tensor_tensor(x1[:, b], x_sb[:, b], bo_b[:], ALU.add)
            last.then_inc(s_init, 1)
            dve.wait_ge(s_qh, 1)
            V.tensor_tensor(qTl[:], cols(4), qTh[:], ALU.subtract).then_inc(s_ql, 1)
            for j in range(PAIRS):
                lo_n(0, 0, j)
            dve.wait_ge(s_init, 3)
            reference_max(0, 0)
            for c in range(DC):
                lo_t(1, 1, c)

            def step(g, par, more_t=True, more=True):
                for j in (0, 1):
                    prob_lo(g, j)
                if more_t:
                    for c in (0, 1, 2):
                        lo_t(g + 2, par, c)
                for j in (2, 3):
                    prob_lo(g, j)
                if more_t:
                    lo_t(g + 2, par, 3)
                if more:
                    reference_max(g + 1, 1 - par)
                    for j in range(PAIRS):
                        lo_n(g + 1, 1 - par, j)
                accumulate(g, par)

            step(0, 0)
            with dve.Fori(0, (NG - 4) // 2) as i:
                step(2 * i + 1, 1)
                step(2 * i + 2, 0)
            step(NG - 3, 1)
            step(NG - 2, 0, more_t=False)
            step(NG - 1, 1, more_t=False, more=False)

            def split_lo(e, par, k):
                dve.wait_ge(s_whi, PIECES * e + k + 1)
                V.scalar_tensor_tensor(wl[:, par, k], wraw[:, k % RAW], WSC, wh[:, par, k],
                                       ALU.mult, ALU.subtract).then_inc(s_wlo, 1)

            steps = [0]

            def done(ins):
                steps[0] += 1
                ins.then_inc(s_mid, 1)
                dve.wait_ge(s_mid, steps[0])

            dve.wait_ge(s_den, 2 * NG)
            done(V.reciprocal(rden[:], den[:]))
            dve.wait_ge(s_acc, 2 * NG)
            for b in range(TB):
                last = V.tensor_scalar(acc[:, b], acc[:, b], rden[:, b:b + 1], None, ALU.mult)
            last.then_inc(s_ev, 1)
            done(V.memset(xpad[:, :, 0:TAPS - 1], 0.0))
            dve.wait_ge(s_pe, 4)
            V.tensor_copy(t1[:], cols(0)).then_inc(s_ev, 1)
            for k in range(4):
                split_lo(0, 0, k)
            dve.wait_ge(s_pe, 6)
            done(V.tensor_tensor(x1[:], x1[:], ps[:, 4:6, :], ALU.add))
            norm(1, x1, acc)
            dve.wait_ge(s_pe, 7)
            V.tensor_copy(xpad[:, :, TAPS - 1:], cols(0)).then_inc(s_ev, 1)
            dve.wait_ge(s_ev, 5)
            for j in range(1, TAPS):
                for c in range(DC):
                    src = xpad[:, c, TAPS - 1 - j:TAPS - 1 - j + TOK]
                    tap = table_sb[:, c, j:j + 1]
                    if j == 1:
                        last = V.tensor_scalar(t1[:, c], src, tap, None, ALU.mult)
                    else:
                        dve.wait_ge(s_zero, DC * (j - 2) + c + 1)
                        last = V.scalar_tensor_tensor(t1[:, c], src, tap, t1[:, c], ALU.mult, ALU.add)
                    last.then_inc(s_zero, 1)
            for b in range(TB):
                last = V.tensor_tensor(x1[:, b], x1[:, b], bias_b[:], ALU.add)
            done(last)
            for k in range(4, PIECES):
                split_lo(0, 0, k)
            dve.wait_ge(s_pe, 9)
            done(V.tensor_tensor(macc[:], x1[:], ps[:, 2:4, :], ALU.add))
            norm(2, macc, acc)
            dve.wait_ge(s_qh, 2)
            V.tensor_tensor(xTl[:], cols(0), xTh[:], ALU.subtract).then_inc(s_ql, 1)
            V.tensor_copy(t2[:], cols(0)).then_inc(s_ev, 1)
            dve.wait_ge(s_pe, 11)
            for b in range(TB):
                last = V.tensor_tensor(logits[:, b], ps[:, 4, NE * b:NE * b + NE], ebias_b[:], ALU.add)
            done(last)
            for b in range(TB):
                last = V.max(top[:, b], logits[:, b])
            done(last)
            for b in range(TB):
                last = V.max_index(topi[:, b], top[:, b], logits[:, b])
            done(last)
            done(V.tensor_copy(topf[:], topi[:]))
            V.tensor_tensor(pr[:, :, 0:1], top[:, :, 1:2], top[:, :, 0:1], ALU.subtract).then_inc(s_gap, 1)
            dve.wait_ge(s_std, 4)
            done(V.tensor_scalar(pr[:, :, 2:3], pr[:, :, 1:2], WSC * WSC, WSC * WSC, ALU.mult, ALU.add))
            done(V.reciprocal(pr[:, :, 2:3], pr[:, :, 2:3]))
            done(V.tensor_tensor(pr[:, :, 3:4], pr[:, :, 1:2], pr[:, :, 2:3], ALU.mult))
            dve.wait_ge(s_iota, 2)
            for b in range(TB):
                for r in range(2):
                    last = V.tensor_scalar(sel[:, b, r], iota8[:], topf[:, b, r:r + 1], pr[:, b, 2 + r:3 + r],
                                           ALU.is_equal, ALU.mult)
            done(last)
            done(V.tensor_tensor(comb[:, :, NS:NX], sel[:, :, 0], sel[:, :, 1], ALU.add))

            def product(i, slot):
                dve.wait_ge(s_sil, i + 1)
                need(dve, s_hl, i - 1)
                V.tensor_tensor(hf[:, slot % 2], sil[:, slot % 2], ps[:, slot, TOK:2 * TOK], ALU.mult)\
                    .then_inc(s_h, 1)

            def hidden_lo(i, slot):
                dve.wait_ge(s_hh, i + 1)
                V.tensor_tensor(hl[:, slot], hf[:, slot % 2], hh[:, slot], ALU.subtract).then_inc(s_hl, 1)

            def combine(e, par):
                for b in range(TB):
                    if b == 0:
                        dve.wait_ge(s_Y, e + 1)
                    else:
                        dve.wait_ge(s_h2, HB * e + HB)
                    need(dve, s_macc, TB * e)
                    w = comb[:, b, e:e + 1] if isinstance(e, int) else comb[:, b, bass.ds(e, 1)]
                    V.scalar_tensor_tensor(macc[:, b], ps[:, 4 + 2 * par + b, :], w, macc[:, b],
                                           ALU.mult, ALU.add).then_inc(s_macc, 1)

            def expert(e, par, more=True, prev=True):
                for b in range(HB):
                    i = HB * e + b
                    product(i, b % 4)
                    if prev and b == 2:
                        combine(e - 1, 1 - par)
                    if more and b >= 2:
                        split_lo(e + 1, 1 - par, b - 2)
                    hidden_lo(i, b % 4)

            expert(0, 0, prev=False)
            with dve.Fori(0, (NX - 2) // 2) as i:
                expert(2 * i + 1, 1)
                expert(2 * i + 2, 0)
            expert(NX - 1, 1, more=False)
            combine(NX - 1, 1)

        @block.tensor
        def _(pe):
            mm = nc.tensor.matmul

            def transpose_rows(bank, src):
                for c in range(DC):
                    for b in range(TB):
                        last = nc.tensor.transpose(cols(bank)[:, c, b * P:(b + 1) * P], src[:, b, c * P:(c + 1) * P],
                                                   ident[:])
                last.then_inc(s_pe, 1)

            def project_t(bank, w, src):
                for o in range(DC):
                    for c in range(DC):
                        last = mm(cols(bank)[:, o], wts[:, w, c, o * P:(o + 1) * P], src[:, c],
                                  start=(c == 0), stop=(c == DC - 1))
                last.then_inc(s_pe, 1)

            def project(bank, w, src, first=True, final=True):
                for b in range(TB):
                    for c in range(DC):
                        last = mm(ps[:, bank + b, :], src(c, b), wts[:, w, c, :],
                                  start=(first and c == 0), stop=(final and c == DC - 1))
                last.then_inc(s_pe, 1)

            def scores(n, par, b):
                for c in range(DC):
                    for q, k in ((qTh, cTh), (qTh, cTl), (qTl, cTh)):
                        for h in range(2):
                            last = mm(psS[:, 2 * b + h, 0:HALF], q[:, c, b * P:(b + 1) * P],
                                      k[:, par, c, h * HALF:(h + 1) * HALF],
                                      start=(c == 0 and q is qTh and k is cTh), stop=(c == DC - 1 and q is qTl))
                last.then_inc(s_S, 1)

            def transposes(g, j):
                a, b = PAIR_TILES[j]
                for t in range(a, b):
                    for q in range(TB):
                        last = nc.tensor.transpose(psT[:, j % 2, (t - a) * TOK + q * P:(t - a) * TOK + (q + 1) * P],
                                                   prob[:, q, t * P:(t + 1) * P], ident[:])
                last.then_inc(s_T, 1)

            pe.wait_ge(s_ident, 2)
            pe.wait_ge(s_ln, 6)
            transpose_rows(4, xn)
            pe.wait_ge(s_ev, 1)
            pe.wait_ge(s_wqk, 32)
            project_t(6, 0, xnT)
            pe.wait_ge(s_ev, 2)
            project_t(4, 1, qpT)
            pe.wait_ge(s_qh, 1)
            pe.wait_ge(s_ql, 1)
            pe.wait_ge(s_hiT, 4)
            pe.wait_ge(s_loT, 4)
            for b in range(TB):
                scores(0, 0, b)

            def step(g, par, more=True):
                pe.wait_ge(s_exp, 2 * g + 2)
                need(pe, s_ptl, PAIRS * g)
                for j in (0, 1):
                    transposes(g, j)
                if more:
                    pe.wait_ge(s_hiT, 4 * g + 8)
                    pe.wait_ge(s_loT, 4 * g + 8)
                    scores(g + 1, 1 - par, 0)
                for j in (2, 3):
                    pe.wait_ge(s_ptl, PAIRS * g + j - 1)
                    transposes(g, j)
                if more:
                    scores(g + 1, 1 - par, 1)
                pe.wait_ge(s_hiN, 4 * g + 4)
                pe.wait_ge(s_loN, 4 * g + 4)
                need(pe, s_acc, 2 * g)
                for b in range(TB):
                    for t in range(KT):
                        if b == 0 and t % 2 == 0:
                            pe.wait_ge(s_pth, PAIRS * g + t // 2 + 1)
                            pe.wait_ge(s_ptl, PAIRS * g + t // 2 + 1)
                        for p, k in ((pTh, cNh), (pTh, cNl), (pTl, cNh)):
                            last = mm(psO[:, b, :], p[:, t, b * P:(b + 1) * P], k[:, par, t],
                                      start=(t == 0 and p is pTh and k is cNh), stop=(t == KT - 1 and p is pTl))
                    last.then_inc(s_PV, 1)

            step(0, 0)
            with pe.Fori(0, (NG - 4) // 2) as i:
                step(2 * i + 1, 1)
                step(2 * i + 2, 0)
            step(NG - 3, 1)
            step(NG - 2, 0)
            step(NG - 1, 1, more=False)

            pe.wait_ge(s_ev, 3)
            transpose_rows(0, acc)
            pe.wait_ge(s_ev, 4)
            pe.wait_ge(s_wvo, 32)
            project_t(2, 0, t1)
            pe.wait_ge(s_zt, DC)
            project(4, 1, lambda c, b: t2[:, c, b * P:(b + 1) * P])
            pe.wait_ge(s_ln, 12)
            transpose_rows(0, acc)
            pe.wait_ge(s_ev, 5)
            pe.wait_ge(s_w12, 32)
            for b in range(TB):
                for c in range(DC):
                    last = mm(ps[:, 2 + b, :], xpad[:, c, TAPS - 1 + b * P:TAPS - 1 + (b + 1) * P], wts[:, 2, c, :],
                              start=(c == 0), stop=False)
            last.then_inc(s_pe, 1)
            for c in range(DC):
                pe.wait_ge(s_zero, DC * (TAPS - 2) + c + 1)
                for b in range(TB):
                    last = mm(ps[:, 2 + b, :], t1[:, c, b * P:(b + 1) * P], wts[:, 3, c, :],
                              start=False, stop=(c == DC - 1))
            last.then_inc(s_pe, 1)
            pe.wait_ge(s_ln, 18)
            transpose_rows(0, acc)
            pe.wait_ge(s_ev, 6)
            for b in range(TB):
                for c in range(DC):
                    last = mm(ps[:, 4, NE * b:NE * b + NE], t2[:, c, b * P:(b + 1) * P], router_sb[:, c],
                              start=(c == 0), stop=(c == DC - 1))
            last.then_inc(s_pe, 1)
            pe.wait_ge(s_qh, 2)
            pe.wait_ge(s_ql, 2)

            def first(e, par, b):
                i = HB * e + b
                if b == 0:
                    pe.wait_ge(s_whi, PIECES * e + 4)
                    pe.wait_ge(s_wlo, PIECES * e + 4)
                need(pe, s_h, i - 3)
                for m in range(2):
                    for c in range(DC):
                        for w, xt in ((wh, xTh), (wh, xTl), (wl, xTh)):
                            last = mm(ps[:, b % 4, m * TOK:(m + 1) * TOK], w13(w, par, m)[:, c, b * P:(b + 1) * P],
                                      xt[:, c], start=(c == 0 and w is wh and xt is xTh),
                                      stop=(c == DC - 1 and w is wl))
                last.then_inc(s_H, 1)

            def second(e, par, b):
                i = HB * e + b
                if b == 0:
                    pe.wait_ge(s_whi, PIECES * e + PIECES)
                    pe.wait_ge(s_wlo, PIECES * e + PIECES)
                    need(pe, s_macc, TB * e - TB)
                pe.wait_ge(s_hh, i + 1)
                pe.wait_ge(s_hl, i + 1)
                for q in range(TB):
                    for h, w in ((hh, wh), (hh, wl), (hl, wh)):
                        last = mm(ps[:, 4 + 2 * par + q, :], h[:, b % 4, q * P:(q + 1) * P], w2(w, par)[:, b],
                                  start=(b == 0 and h is hh and w is wh), stop=(b == HB - 1 and h is hl))
                    if b == HB - 1 and q == 0:
                        last.then_inc(s_Y, 1)
                last.then_inc(s_h2, 1)

            def expert(e, par, more=True):
                for b in range(2, HB + 2):
                    if b < HB:
                        first(e, par, b)
                    elif more:
                        first(e + 1, 1 - par, b - HB)
                    second(e, par, b - 2)

            first(0, 0, 0)
            first(0, 0, 1)
            expert(0, 0)
            expert(1, 1)
            with pe.Fori(1, NX // 2 - 1) as i:
                expert(2 * i, 0)
                expert(2 * i + 1, 1)
            expert(NX - 2, 0)
            expert(NX - 1, 1, more=False)


def kernel(**inputs):
    import numpy as np
    import concourse.bacc as bacc
    from concourse.bass_utils import run_bass_kernel_spmd

    a = {name: np.asarray(v) for name, v in inputs.items()}

    def chunks(w):
        return w.reshape(DC, P, -1).transpose(1, 0, 2)

    def piece(w):
        return w.reshape(-1, P, w.shape[1]).transpose(1, 0, 2).reshape(P, -1)

    f = "L0_ffn_"
    experts = [(a[f + "sw1"][i], a[f + "sw3"][i], a[f + "sw2"][i]) for i in range(NS)]
    experts += [(a[f + "w1"][i], a[f + "w3"][i], a[f + "w2"][i]) for i in range(NE)]
    ctx = a["ctx_1024"].reshape(NG, P, KT, DC, P)
    arrays = {
        "x": a["x"],
        "ctx_nat": ctx.reshape(NG, P, KT, D),
        "ctx_t": ctx.transpose(0, 4, 3, 2, 1).reshape(NG, P, DC, GK),
        "wmats": np.stack([chunks(a["L0_xattn_Wq"].T), chunks(a["L0_xattn_Wk"]), chunks(a["L0_xattn_Wv"].T),
                           chunks(a["L0_xattn_Wo"].T), chunks(a["L0_attn_W1"]), chunks(a["L0_attn_W2"])]),
        "bq": a["L0_xattn_bq"].reshape(DC, P).T,
        "bv": a["L0_xattn_bv"].reshape(DC, P).T,
        "bo": a["L0_xattn_bo"],
        "bias": a["L0_attn_bias"],
        "table": chunks(a["L0_attn_embeddings_table"].T),
        "router": chunks(a[f + "router_w"].T),
        "ebias": a[f + "expert_bias"],
        "wexp": np.stack([np.concatenate([piece(w1.T), piece(w3.T), piece(w2.T)], axis=1) for w1, w3, w2 in experts]),
    }
    nc = bacc.Bacc("TRN2", target_bir_lowering=False, num_devices=1)
    args, ins = [], {}
    for name, v in arrays.items():
        ins[f"{name}_dram"] = np.ascontiguousarray(v)
        args.append(nc.dram_tensor(f"{name}_dram", v.shape, mybir.dt.from_np(v.dtype), kind="ExternalInput").ap())
    args.append(nc.dram_tensor("out_dram", a["x"].shape, F32, kind="ExternalOutput").ap())
    perceiver_kernel(nc, *args)
    r = run_bass_kernel_spmd(nc, [ins], core_ids=[0])
    return r.results[0]["out_dram"]
```

```python
from contextlib import ExitStack
import math

import concourse.bass as bass
from concourse import mybir

P = 128
F32 = mybir.dt.float32
F16 = mybir.dt.float16
U32 = mybir.dt.uint32
ALU = mybir.AluOpType
ACT = mybir.ActivationFunctionType
AX = mybir.AxisListType

D = 512
DC = D // P
TOK = 256
TB = TOK // P
KEYS = 25088
KT = 7
GK = KT * P
NG = KEYS // GK
HALF = GK // 2
PAIRS = 4
TAPS = 21
NE = 8
NS = 2
NX = NS + NE
ND = NS + 3
NC = NX - ND
HID = 1024
HB = HID // P
HH = HID // 2
PIECE = 2048
PIECES = 3 * 4096 // PIECE
RAW = 3
SC = 1.0 / math.sqrt(D)
LN_P = 12 * math.log(2.0)
WSC = 64.0
EPS = 1e-5


def need(eng, sem, count):
    if not (isinstance(count, int) and count <= 0):
        eng.wait_ge(sem, count)


def perceiver_kernel(nc, x, ctx_nat, ctx_t, wmats, bq, bv, bo, bias, table, router, ebias, wexp, out):
    with ExitStack() as keep:
        def sb(name, shape, dt, stack=keep):
            return stack.enter_context(nc.sbuf_tensor(name, shape, dt))

        def sem(name):
            return keep.enter_context(nc.semaphore(name))

        ident = sb("ident", [P, P], F32)
        x_sb = sb("x_sb", [P, TB, D], F32)
        x1 = sb("x1", [P, TB, D], F32)
        acc = sb("acc", [P, TB, D], F32)
        bo_b = sb("bo_b", [P, D], F32)
        bias_b = sb("bias_b", [P, D], F32)
        ebias_b = sb("ebias_b", [P, NE], F32)
        bq_sb = sb("bq_sb", [P, DC], F32)
        bv_sb = sb("bv_sb", [P, DC], F32)
        table_sb = sb("table_sb", [P, DC, TAPS], F32)
        router_sb = sb("router_sb", [P, DC, NE], F32)
        stats = sb("stats", [P, TB, 6], F32)
        mv = sb("mv", [P, TB, 2], F32)
        var_e = sb("var_e", [P, TB], F32)
        std = sb("std", [P, TB], F32)
        rstd = sb("rstd", [P, TB], F32)
        mx = sb("mx", [P, 2, TB], F32)
        cm = sb("cm", [P, TB], F32)
        nb = sb("nb", [P, 2, TB], F32)
        dm = sb("dm", [P, 2, TB], F32)
        alpha = sb("alpha", [P, 2, TB], F32)
        rs = sb("rs", [P, 2, TB], F32)
        den = sb("den", [P, TB], F32)
        rden = sb("rden", [P, TB], F32)
        iota8 = sb("iota8", [P, NE], F32)
        iota_s = sb("iota_s", [P, P], F32)
        ones16 = sb("ones16", [P, P], F16)
        before16 = sb("before16", [P, P], F16)
        ident16 = sb("ident16", [P, P], F16)
        logits = sb("logits", [P, TB, NE], F32)
        top = sb("top", [P, TB, 8], F32)
        topi = sb("topi", [P, TB, 8], U32)
        topf = sb("topf", [P, TB, 8], F32)
        pr = sb("pr", [P, TB, 4], F32)
        sel = sb("sel", [P, TB, 2, NE], F32)
        cbase = sb("cbase", [P, TB, NE], F32)
        comb = sb("comb", [P, TB, NX], F32)
        second16 = sb("second16", [P, TB, NE], F16)
        chosen16 = sb("chosen16", [P, TB, NE], F16)
        load = sb("load", [P, NE], F32)
        load_top = sb("load_top", [P, NE], F32)
        order = sb("order", [P, NE], U32)
        order_f = sb("order_f", [P, NE], F32)
        picked = sb("picked", [P, TB, NE, NE], F32)
        mine = sb("mine", [P, TB, NC], F32)
        mine16 = sb("mine16", [P, TB, NC], F16)
        slot = sb("slot", [P, TB, NC], F32)

        old = ExitStack()
        wts = sb("wts", [P, 4, DC, D], F32, old)
        old.close()
        place = sb("place", [P, NC, TB, P], F16)
        placeT = sb("placeT", [P, NC, TOK], F16)
        xnh = sb("xnh", [P, TB, D], F16)
        xnl = sb("xnl", [P, TB, D], F16)
        xgh = sb("xgh", [P, DC, P], F16)
        xgl = sb("xgl", [P, DC, P], F16)
        csil = sb("csil", [P, 2, HH], F32)
        ch = sb("ch", [P, 2, HH], F32)
        chh = sb("chh", [P, HB, P], F16)
        chl = sb("chl", [P, HB, P], F16)
        yh = sb("yh", [P, D], F16)
        yl = sb("yl", [P, D], F16)
        used = 2 * (NC * TB * P + NC * TOK + 2 * TB * D + 2 * DC * P + 2 * HB * P + 2 * D) + 4 * 4 * HH
        rest = sb("rest", [P, (4 * DC * D * 4 - used) // 4], F32)

        att = ExitStack()
        rawT = sb("rawT", [P, 2, DC, GK], F32, att)
        rawN = sb("rawN", [P, 2, KT, D], F32, att)
        cTh = sb("cTh", [P, 2, DC, GK], F16, att)
        cTl = sb("cTl", [P, 2, DC, GK], F16, att)
        cNh = sb("cNh", [P, 2, KT, D], F16, att)
        cNl = sb("cNl", [P, 2, KT, D], F16, att)
        prob = sb("prob", [P, TB, GK], F32, att)
        pTh = sb("pTh", [P, KT, TOK], F16, att)
        pTl = sb("pTl", [P, KT, TOK], F16, att)
        qTh = sb("qTh", [P, DC, TOK], F16, att)
        qTl = sb("qTl", [P, DC, TOK], F16, att)
        att.close()
        wraw = sb("wraw", [P, RAW, PIECE], F32)
        wh = sb("wh", [P, 2, PIECES, PIECE], F16)
        wl = sb("wl", [P, 2, PIECES, PIECE], F16)
        t1 = sb("t1", [P, DC, TOK], F32)
        t2 = sb("t2", [P, DC, TOK], F32)
        xpad = sb("xpad", [P, DC, TAPS - 1 + TOK], F32)
        macc = sb("macc", [P, TB, D], F32)
        xTh = sb("xTh", [P, DC, TOK], F16)
        xTl = sb("xTl", [P, DC, TOK], F16)
        sil = sb("sil", [P, 2, TOK], F32)
        hf = sb("hf", [P, 2, TOK], F32)
        hh = sb("hh", [P, 4, TOK], F16)
        hl = sb("hl", [P, 4, TOK], F16)

        xn = prob[:, :, 0:D]
        xnT = rawN[:, 1, 0:2, :].rearrange("p a (b t) -> p (a b) t", t=TOK)
        qpT = rawN[:, 1, 2:4, :].rearrange("p a (b t) -> p (a b) t", t=TOK)

        ps = keep.enter_context(nc.psum_tensor("ps", [P, 8, 512], F32))
        psS = ps[:, 0:4, :]
        psT = ps[:, 4:6, :]
        psO = ps[:, 6:8, :]

        def cols(bank):
            return ps[:, bank:bank + 2, :].rearrange("p a (b t) -> p (a b) t", t=TOK)

        def w13(t, par, m):
            return t[:, par, 2 * m:2 * m + 2, :].rearrange("p a (c h) -> p (a c) h", h=HID)

        def w2(t, par):
            return t[:, par, 4:6, :].rearrange("p a (c n) -> p (a c) n", n=D)

        s_x = sem("s_x")
        s_wqk = sem("s_wqk")
        s_small = sem("s_small")
        s_wvo = sem("s_wvo")
        s_w12 = sem("s_w12")
        s_rawT = [sem(f"s_rawT{i}") for i in range(2)]
        s_rawN = [sem(f"s_rawN{i}") for i in range(2)]
        s_ident = sem("s_ident")
        s_iota = sem("s_iota")
        s_init = sem("s_init")
        s_ln = sem("s_ln")
        s_std = sem("s_std")
        s_pe = sem("s_pe")
        s_ev = sem("s_ev")
        s_qh = sem("s_qh")
        s_ql = sem("s_ql")
        s_hiT = sem("s_hiT")
        s_loT = sem("s_loT")
        s_hiN = sem("s_hiN")
        s_loN = sem("s_loN")
        s_S = sem("s_S")
        s_cm = sem("s_cm")
        s_mx = sem("s_mx")
        s_ref = sem("s_ref")
        s_alpha = sem("s_alpha")
        s_exp = sem("s_exp")
        s_T = sem("s_T")
        s_pth = sem("s_pth")
        s_ptl = sem("s_ptl")
        s_PV = sem("s_PV")
        s_acc = sem("s_acc")
        s_den = sem("s_den")
        s_mid = sem("s_mid")
        s_zt = sem("s_zt")
        s_zero = sem("s_zero")
        s_gap = sem("s_gap")
        s_gexp = sem("s_gexp")
        s_xnh = sem("s_xnh")
        s_xnl = sem("s_xnl")
        s_chosen = sem("s_chosen")
        s_load = sem("s_load")
        s_order = sem("s_order")
        s_mine = sem("s_mine")
        s_slot = sem("s_slot")
        s_place = sem("s_place")
        s_placeT = sem("s_placeT")
        s_placed = sem("s_placed")
        s_xg = sem("s_xg")
        s_xgh = sem("s_xgh")
        s_xgl = sem("s_xgl")
        s_c1 = sem("s_c1")
        s_csil = sem("s_csil")
        s_cp = sem("s_cp")
        s_cT = sem("s_cT")
        s_chh = sem("s_chh")
        s_chl = sem("s_chl")
        s_cY = sem("s_cY")
        s_yh = sem("s_yh")
        s_yl = sem("s_yl")
        s_cs = sem("s_cs")
        s_wraw = [sem(f"s_wraw{i}") for i in range(RAW)]
        s_whi = sem("s_whi")
        s_wlo = sem("s_wlo")
        s_H = sem("s_H")
        s_sil = sem("s_sil")
        s_h = sem("s_h")
        s_hh = sem("s_hh")
        s_hl = sem("s_hl")
        s_h2 = sem("s_h2")
        s_Y = sem("s_Y")
        s_macc = sem("s_macc")
        s_out = sem("s_out")

        PAIR_TILES = [(0, 2), (2, 4), (4, 6), (6, 7)]
        tok_view = lambda a: a.rearrange("o (b p) d -> p (o b) d", p=P)

        block = keep.enter_context(nc.Block())

        @block.sync
        def _(sp):
            sp.dma_start(x_sb[:], tok_view(x)).then_inc(s_x, 16)
            for m in range(2):
                sp.dma_start(wts[:, m], wmats[m]).then_inc(s_wqk, 16)
            small = [(bq_sb[:], bq), (bv_sb[:], bv), (table_sb[:], table), (router_sb[:], router),
                     (bo_b[:], bo.partition_broadcast(P)), (bias_b[:], bias.partition_broadcast(P)),
                     (ebias_b[:], ebias.partition_broadcast(P))]
            for dst, src in small:
                sp.dma_start(dst, src).then_inc(s_small, 16)

            def load_t(g, slot):
                sp.dma_start(rawT[:, slot], ctx_t[g]).then_inc(s_rawT[slot], 16)

            def load_n(g, slot):
                sp.dma_start(rawN[:, slot], ctx_nat[g]).then_inc(s_rawN[slot], 16)

            def split_t(count):
                sp.wait_ge(s_hiT, 4 * count)
                sp.wait_ge(s_loT, 4 * count)

            def split_n(count):
                sp.wait_ge(s_hiN, 4 * count)
                sp.wait_ge(s_loN, 4 * count)

            load_t(0, 0)
            load_n(0, 0)
            load_t(1, 1)
            split_t(1)
            load_t(2, 0)
            sp.wait_ge(s_qh, 1)
            sp.wait_ge(s_ql, 1)
            load_n(1, 1)
            split_t(2)
            load_t(3, 1)
            split_n(1)
            load_n(2, 0)
            for m in range(2):
                sp.dma_start(wts[:, m], wmats[2 + m]).then_inc(s_wvo, 16)
            for m in range(2):
                sp.dma_start(wts[:, 2 + m], wmats[4 + m]).then_inc(s_w12, 16)
            with sp.Fori(2, NG // 2) as i:
                split_t(2 * i - 1)
                load_t(2 * i, 0)
                split_n(2 * i - 2)
                load_n(2 * i - 1, 1)
                split_t(2 * i)
                load_t(2 * i + 1, 1)
                split_n(2 * i - 1)
                load_n(2 * i, 0)
            split_n(NG - 2)
            load_n(NG - 1, 1)

            def load_piece(e, k):
                sp.dma_start(wraw[:, k % RAW], wexp[e, :, k * PIECE:(k + 1) * PIECE]).then_inc(s_wraw[k % RAW], 16)

            split_t(NG)
            for k in range(RAW):
                load_piece(0, k)
            for k in range(RAW, PIECES):
                sp.wait_ge(s_wlo, k - RAW + 1)
                load_piece(0, k)
            for k in range(PIECES):
                sp.wait_ge(s_wlo, PIECES + k - RAW + 1)
                load_piece(1, k)
            sp.wait_ge(s_order, 1)
            with sp.Fori(NS, NX) as e:
                routed = sp.value_load(order[0:1, bass.ds(e - NS, 1)], min_val=0, max_val=NE - 1)
                for k in range(PIECES):
                    sp.wait_ge(s_wlo, PIECES * e + k - RAW + 1)
                    load_piece(routed + NS, k)
            for b in range(TB):
                sp.wait_ge(s_macc, TB * NX - TB + b + 1)
                sp.dma_start(tok_view(out)[:, b, :], macc[:, b, :]).then_inc(s_out, 16)
            sp.wait_ge(s_out, 16 * TB)

        @block.gpsimd
        def _(pool):
            nc.gpsimd.memset(ident[:], 0.0).then_inc(s_ident, 1)
            pool.wait_ge(s_ident, 1)
            nc.gpsimd.affine_select(out=ident[:], in_=ident[:], compare_op=ALU.not_equal, fill=1.0, base=0,
                                    pattern=[[-1, P]], channel_multiplier=1).then_inc(s_ident, 1)
            nc.gpsimd.iota(iota8[:], pattern=[[1, NE]], base=0, channel_multiplier=0,
                           allow_small_or_imprecise_dtypes=True).then_inc(s_iota, 1)
            nc.gpsimd.memset(comb[:, :, 0:NS], 1.0 / (WSC * WSC)).then_inc(s_iota, 1)
            nc.gpsimd.iota(iota_s[:], pattern=[[1, P]], base=0, channel_multiplier=0,
                           allow_small_or_imprecise_dtypes=True).then_inc(s_iota, 1)
            nc.gpsimd.memset(ones16[:], 1.0).then_inc(s_iota, 1)
            pool.wait_ge(s_iota, 4)
            nc.gpsimd.affine_select(out=before16[:], in_=ones16[:], compare_op=ALU.is_gt, fill=0.0, base=0,
                                    pattern=[[1, P]], channel_multiplier=-1).then_inc(s_iota, 1)
            pool.wait_ge(s_ident, 2)
            nc.gpsimd.tensor_copy(ident16[:], ident[:]).then_inc(s_iota, 1)

        @block.scalar
        def _(act):
            def root(n):
                act.wait_ge(s_ln, 6 * n + 4)
                nc.scalar.activation(std[:], var_e[:], ACT.Sqrt).then_inc(s_std, 1)

            def hi_t(g, par, c):
                nc.scalar.activation(cTh[:, par, c], rawT[:, par, c], ACT.Copy).then_inc(s_hiT, 1)

            def hi_n(par, j):
                a, b = PAIR_TILES[j]
                nc.scalar.activation(cNh[:, par, a:b], rawN[:, par, a:b], ACT.Copy).then_inc(s_hiN, 1)

            def landed(sems, g, par):
                act.wait_ge(sems[par], (g - par) * 8 + 16)

            def softmax(n, par):
                act.wait_ge(s_ref, 2 * n + 2)
                need(act, s_acc, 2 * n - 2)
                nc.scalar.activation(alpha[:, par, :], dm[:, par, :], ACT.Exp, scale=SC).then_inc(s_alpha, 1)
                need(act, s_T, PAIRS * n)
                for b in range(TB):
                    nc.scalar.activation(prob[:, b].rearrange("p (h k) -> p h k", h=2), psS[:, 2 * b:2 * b + 2, 0:HALF],
                                         ACT.Exp, bias=nb[:, par, b:b + 1], scale=SC,
                                         accum_out=rs[:, par, b:b + 1]).then_inc(s_exp, 1)

            def prob_hi(g, j):
                a, b = PAIR_TILES[j]
                act.wait_ge(s_T, PAIRS * g + j + 1)
                nc.scalar.activation(pTh[:, a:b], psT[:, j % 2, 0:(b - a) * TOK].rearrange("p (a t) -> p a t", t=TOK),
                                     ACT.Copy).then_inc(s_pth, 1)

            root(0)
            landed(s_rawT, 0, 0)
            for c in range(DC):
                hi_t(0, 0, c)
            act.wait_ge(s_pe, 3)
            nc.scalar.activation(qTh[:], cols(4), ACT.Copy).then_inc(s_qh, 1)
            landed(s_rawN, 0, 0)
            for j in range(PAIRS):
                hi_n(0, j)
            landed(s_rawT, 1, 1)
            for c in range(DC):
                hi_t(1, 1, c)
            softmax(0, 0)

            def step(g, par, more_t=True, more=True):
                need(act, s_PV, 2 * g)
                for j in (0, 1):
                    prob_hi(g, j)
                if more_t:
                    landed(s_rawT, g + 2, par)
                    act.wait_ge(s_S, 2 * g + 2)
                    for c in range(DC):
                        hi_t(g + 2, par, c)
                for j in (2, 3):
                    prob_hi(g, j)
                if more:
                    landed(s_rawN, g + 1, 1 - par)
                    for j in (0, 1):
                        hi_n(1 - par, j)
                    softmax(g + 1, 1 - par)
                    for j in (2, 3):
                        hi_n(1 - par, j)

            step(0, 0)
            with act.Fori(0, (NG - 4) // 2) as i:
                step(2 * i + 1, 1)
                step(2 * i + 2, 0)
            step(NG - 3, 1)
            step(NG - 2, 0, more_t=False)
            step(NG - 1, 1, more_t=False, more=False)

            def split_hi(e, par, k):
                act.wait_ge(s_wraw[k % RAW], 32 * e + 16 * (k // RAW) + 16)
                nc.scalar.activation(wh[:, par, k], wraw[:, k % RAW], ACT.Copy, scale=WSC).then_inc(s_whi, 1)

            act.wait_ge(s_PV, 2 * NG)
            for k in range(4):
                split_hi(0, 0, k)
            act.wait_ge(s_pe, 5)
            for c in range(DC):
                nc.scalar.activation(t2[:, c], cols(2)[:, c], ACT.Identity, bias=bv_sb[:, c:c + 1]).then_inc(s_zt, 1)
            root(1)
            for k in range(4, PIECES):
                split_hi(0, 0, k)
            root(2)
            act.wait_ge(s_pe, 10)
            nc.scalar.activation(xTh[:], cols(0), ACT.Copy).then_inc(s_qh, 1)
            def silu(i, slot):
                act.wait_ge(s_H, i + 1)
                need(act, s_h, i - 1)
                nc.scalar.activation(sil[:, slot % 2], ps[:, slot, 0:TOK], ACT.Silu, scale=1.0 / WSC).then_inc(s_sil, 1)

            def hidden_hi(i, slot):
                act.wait_ge(s_h, i + 1)
                need(act, s_h2, i - 3)
                nc.scalar.activation(hh[:, slot], hf[:, slot % 2], ACT.Copy).then_inc(s_hh, 1)

            def expert(e, par):
                for b in range(HB):
                    i = HB * e + b
                    silu(i, b % 4)
                    if (e, b) == (0, 0):
                        act.wait_ge(s_gap, 1)
                        nc.scalar.activation(pr[:, :, 1:2], pr[:, :, 0:1], ACT.Exp).then_inc(s_gexp, 1)
                    if (e, b) == (0, 1):
                        nc.scalar.activation(xnh[:], acc[:], ACT.Copy).then_inc(s_xnh, 1)
                    if b >= 2:
                        if b == 2:
                            need(act, s_h2, HB * e)
                        split_hi(e + 1, 1 - par, b - 2)
                    hidden_hi(i, b % 4)

            for e in range(ND):
                expert(e, e % 2)

            def gathered_hi(r, bank):
                act.wait_ge(s_xg, r + 1)
                nc.scalar.activation(xgh[:], ps[:, bank, :].rearrange("p (c t) -> p c t", t=P), ACT.Copy)\
                    .then_inc(s_xgh, 1)

            def gathered(r):
                e, par = ND + r, (ND + r) % 2

                def half(h):
                    act.wait_ge(s_c1, 2 * r + h + 1)
                    need(act, s_cp, 2 * (r - 1) + h + 1)
                    nc.scalar.activation(csil[:, h], ps[:, 2 * h, :], ACT.Silu, scale=1.0 / WSC).then_inc(s_csil, 1)

                def hidden(h):
                    act.wait_ge(s_cT, 2 * r + h + 1)
                    nc.scalar.activation(chh[:, 4 * h:4 * h + 4], ps[:, 4 + h, :].rearrange("p (c t) -> p c t", t=P),
                                         ACT.Copy).then_inc(s_chh, 1)

                def split(k):
                    if r < NC - 1:
                        split_hi(e + 1, 1 - par, k)

                if r == 0:
                    act.wait_ge(s_h2, HB * ND)
                else:
                    act.wait_ge(s_cY, r)
                split(0)
                split(1)
                half(0)
                split(2)
                hidden(0)
                split(3)
                half(1)
                split(4)
                hidden(1)
                if r < NC - 1:
                    gathered_hi(r + 1, 4)
                split(5)
                act.wait_ge(s_cY, r + 1)
                nc.scalar.activation(yh[:], ps[:, 6, :], ACT.Copy, scale=1.0 / WSC).then_inc(s_yh, 1)

            gathered_hi(0, 6)
            for r in range(NC):
                gathered(r)

        @block.vector
        def _(dve):
            V = nc.vector

            def norm(n, src, dst):
                for b in range(TB):
                    V.bn_stats(stats[:, b], src[:, b]).then_inc(s_ln, 1)
                dve.wait_ge(s_ln, 6 * n + 2)
                for b in range(TB):
                    last = V.bn_aggr(mv[:, b], stats[:, b])
                last.then_inc(s_ln, 1)
                dve.wait_ge(s_ln, 6 * n + 3)
                V.tensor_scalar(var_e[:], mv[:, :, 1], EPS, None, ALU.add).then_inc(s_ln, 1)
                dve.wait_ge(s_std, n + 1)
                V.reciprocal(rstd[:], std[:]).then_inc(s_ln, 1)
                dve.wait_ge(s_ln, 6 * n + 5)
                for b in range(TB):
                    last = V.tensor_scalar(dst[:, b], src[:, b], mv[:, b, 0:1], rstd[:, b:b + 1],
                                           ALU.subtract, ALU.mult)
                last.then_inc(s_ln, 1)

            def lo_t(g, par, c):
                dve.wait_ge(s_hiT, 4 * g + c + 1)
                V.tensor_tensor(cTl[:, par, c], rawT[:, par, c], cTh[:, par, c], ALU.subtract).then_inc(s_loT, 1)

            def lo_n(g, par, j):
                a, b = PAIR_TILES[j]
                dve.wait_ge(s_hiN, 4 * g + j + 1)
                V.tensor_tensor(cNl[:, par, a:b], rawN[:, par, a:b], cNh[:, par, a:b], ALU.subtract).then_inc(s_loN, 1)

            def reference_max(n, par):
                for b in range(TB):
                    dve.wait_ge(s_S, 2 * n + b + 1)
                    V.tensor_reduce(cm[:, b:b + 1], psS[:, 2 * b:2 * b + 2, 0:HALF], AX.XY, ALU.max).then_inc(s_cm, 1)
                dve.wait_ge(s_cm, 2 * n + 2)
                V.tensor_tensor(mx[:, par], mx[:, 1 - par], cm[:], ALU.max).then_inc(s_mx, 1)
                dve.wait_ge(s_mx, n + 1)
                V.tensor_scalar(nb[:, par], mx[:, par], -SC, LN_P, ALU.mult, ALU.add).then_inc(s_ref, 1)
                V.tensor_tensor(dm[:, par], mx[:, 1 - par], mx[:, par], ALU.subtract).then_inc(s_ref, 1)

            def prob_lo(g, j):
                a, b = PAIR_TILES[j]
                dve.wait_ge(s_pth, PAIRS * g + j + 1)
                V.tensor_tensor(pTl[:, a:b], psT[:, j % 2, 0:(b - a) * TOK].rearrange("p (a t) -> p a t", t=TOK),
                                pTh[:, a:b], ALU.subtract).then_inc(s_ptl, 1)

            def accumulate(g, par):
                dve.wait_ge(s_exp, 2 * g + 2)
                need(dve, s_den, 2 * g)
                for b in range(TB):
                    V.scalar_tensor_tensor(den[:, b:b + 1], den[:, b:b + 1], alpha[:, par, b:b + 1],
                                           rs[:, par, b:b + 1], ALU.mult, ALU.add).then_inc(s_den, 1)
                need(dve, s_acc, 2 * g)
                for b in range(TB):
                    dve.wait_ge(s_PV, 2 * g + b + 1)
                    V.scalar_tensor_tensor(acc[:, b], acc[:, b], alpha[:, par, b:b + 1], psO[:, b],
                                           ALU.mult, ALU.add).then_inc(s_acc, 1)

            V.memset(mx[:], -1e30).then_inc(s_init, 1)
            V.memset(den[:], 0.0).then_inc(s_init, 1)
            V.memset(acc[:], 0.0).then_inc(s_init, 1)
            dve.wait_ge(s_x, 16)
            norm(0, x_sb, xn)
            dve.wait_ge(s_pe, 1)
            V.tensor_copy(xnT, cols(4)).then_inc(s_ev, 1)
            dve.wait_ge(s_pe, 2)
            dve.wait_ge(s_small, 16 * 7)
            for c in range(DC):
                last = V.tensor_scalar(qpT[:, c], cols(6)[:, c], bq_sb[:, c:c + 1], None, ALU.add)
            last.then_inc(s_ev, 1)
            for c in range(DC):
                lo_t(0, 0, c)
            for b in range(TB):
                last = V.tensor_tensor(x1[:, b], x_sb[:, b], bo_b[:], ALU.add)
            last.then_inc(s_init, 1)
            dve.wait_ge(s_qh, 1)
            V.tensor_tensor(qTl[:], cols(4), qTh[:], ALU.subtract).then_inc(s_ql, 1)
            for j in range(PAIRS):
                lo_n(0, 0, j)
            dve.wait_ge(s_init, 3)
            reference_max(0, 0)
            for c in range(DC):
                lo_t(1, 1, c)

            def step(g, par, more_t=True, more=True):
                for j in (0, 1):
                    prob_lo(g, j)
                if more_t:
                    for c in (0, 1, 2):
                        lo_t(g + 2, par, c)
                for j in (2, 3):
                    prob_lo(g, j)
                if more_t:
                    lo_t(g + 2, par, 3)
                if more:
                    reference_max(g + 1, 1 - par)
                    for j in range(PAIRS):
                        lo_n(g + 1, 1 - par, j)
                accumulate(g, par)

            step(0, 0)
            with dve.Fori(0, (NG - 4) // 2) as i:
                step(2 * i + 1, 1)
                step(2 * i + 2, 0)
            step(NG - 3, 1)
            step(NG - 2, 0, more_t=False)
            step(NG - 1, 1, more_t=False, more=False)

            def split_lo(e, par, k):
                dve.wait_ge(s_whi, PIECES * e + k + 1)
                V.scalar_tensor_tensor(wl[:, par, k], wraw[:, k % RAW], WSC, wh[:, par, k],
                                       ALU.mult, ALU.subtract).then_inc(s_wlo, 1)

            steps = [0]

            def done(ins):
                steps[0] += 1
                ins.then_inc(s_mid, 1)
                dve.wait_ge(s_mid, steps[0])

            dve.wait_ge(s_den, 2 * NG)
            done(V.reciprocal(rden[:], den[:]))
            dve.wait_ge(s_acc, 2 * NG)
            for b in range(TB):
                last = V.tensor_scalar(acc[:, b], acc[:, b], rden[:, b:b + 1], None, ALU.mult)
            last.then_inc(s_ev, 1)
            done(V.memset(xpad[:, :, 0:TAPS - 1], 0.0))
            dve.wait_ge(s_pe, 4)
            V.tensor_copy(t1[:], cols(0)).then_inc(s_ev, 1)
            for k in range(4):
                split_lo(0, 0, k)
            dve.wait_ge(s_pe, 6)
            done(V.tensor_tensor(x1[:], x1[:], ps[:, 4:6, :], ALU.add))
            norm(1, x1, acc)
            dve.wait_ge(s_pe, 7)
            V.tensor_copy(xpad[:, :, TAPS - 1:], cols(0)).then_inc(s_ev, 1)
            dve.wait_ge(s_ev, 5)
            for j in range(1, TAPS):
                for c in range(DC):
                    src = xpad[:, c, TAPS - 1 - j:TAPS - 1 - j + TOK]
                    tap = table_sb[:, c, j:j + 1]
                    if j == 1:
                        last = V.tensor_scalar(t1[:, c], src, tap, None, ALU.mult)
                    else:
                        dve.wait_ge(s_zero, DC * (j - 2) + c + 1)
                        last = V.scalar_tensor_tensor(t1[:, c], src, tap, t1[:, c], ALU.mult, ALU.add)
                    last.then_inc(s_zero, 1)
            for b in range(TB):
                last = V.tensor_tensor(x1[:, b], x1[:, b], bias_b[:], ALU.add)
            done(last)
            for k in range(4, PIECES):
                split_lo(0, 0, k)
            dve.wait_ge(s_pe, 9)
            done(V.tensor_tensor(macc[:], x1[:], ps[:, 2:4, :], ALU.add))
            norm(2, macc, acc)
            dve.wait_ge(s_qh, 2)
            V.tensor_tensor(xTl[:], cols(0), xTh[:], ALU.subtract).then_inc(s_ql, 1)
            V.tensor_copy(t2[:], cols(0)).then_inc(s_ev, 1)
            def route_top():
                dve.wait_ge(s_pe, 11)
                for b in range(TB):
                    last = V.tensor_tensor(logits[:, b], ps[:, 6, NE * b:NE * b + NE], ebias_b[:], ALU.add)
                done(last)
                for b in range(TB):
                    last = V.max(top[:, b], logits[:, b])
                done(last)
                V.tensor_tensor(pr[:, :, 0:1], top[:, :, 1:2], top[:, :, 0:1], ALU.subtract).then_inc(s_gap, 1)
                for b in range(TB):
                    last = V.max_index(topi[:, b], top[:, b], logits[:, b])
                done(last)
                done(V.tensor_copy(topf[:], topi[:]))

            def route_weights():
                dve.wait_ge(s_gexp, 1)
                done(V.tensor_scalar(pr[:, :, 2:3], pr[:, :, 1:2], WSC * WSC, WSC * WSC, ALU.mult, ALU.add))
                done(V.reciprocal(pr[:, :, 2:3], pr[:, :, 2:3]))
                done(V.tensor_tensor(pr[:, :, 3:4], pr[:, :, 1:2], pr[:, :, 2:3], ALU.mult))
                dve.wait_ge(s_iota, 2)
                for b in range(TB):
                    for r in range(2):
                        last = V.tensor_scalar(sel[:, b, r], iota8[:], topf[:, b, r:r + 1], pr[:, b, 2 + r:3 + r],
                                               ALU.is_equal, ALU.mult)
                    last = V.tensor_scalar(second16[:, b], iota8[:], topf[:, b, 1:2], None, ALU.is_equal)
                done(last)
                for b in range(TB):
                    last = V.scalar_tensor_tensor(chosen16[:, b], iota8[:], topf[:, b, 0:1], second16[:, b],
                                                  ALU.is_equal, ALU.add)
                last.then_inc(s_chosen, 1)
                done(V.tensor_tensor(cbase[:], sel[:, :, 0], sel[:, :, 1], ALU.add))

            def route_order():
                dve.wait_ge(s_load, 1)
                done(V.tensor_copy(load[:], ps[:, 6, 0:NE]))
                done(V.max(load_top[:], load[:]))
                V.max_index(order[:], load_top[:], load[:]).then_inc(s_order, 1)
                dve.wait_ge(s_order, 1)
                done(V.tensor_copy(order_f[:], order[:]))
                for b in range(TB):
                    for r in range(NE):
                        last = V.scalar_tensor_tensor(picked[:, b, r], iota8[:], order_f[:, r:r + 1], cbase[:, b],
                                                      ALU.is_equal, ALU.mult, accum_out=comb[:, b, NS + r:NS + r + 1])
                done(last)

            def route_mine():
                V.tensor_scalar(mine16[:], comb[:, :, ND:NX], 0.0, None, ALU.is_gt).then_inc(s_mine, 1)
                V.tensor_scalar(mine[:], comb[:, :, ND:NX], 0.0, None, ALU.is_gt).then_inc(s_mine, 1)
                dve.wait_ge(s_mine, 2)
                done(V.tensor_scalar(comb[:, :, ND:NX], comb[:, :, ND:NX], WSC, None, ALU.mult))

            def route_places():
                dve.wait_ge(s_slot, 1)
                done(V.tensor_copy(slot[:], ps[:, 6, 0:TB * NC].rearrange("p (b r) -> p b r", r=NC)))
                dve.wait_ge(s_iota, 3)
                for r in range(NC):
                    for b in range(TB):
                        last = V.tensor_scalar(place[:, r, b], iota_s[:], slot[:, b, r:r + 1], mine[:, b, r:r + 1],
                                               ALU.is_equal, ALU.mult)
                last.then_inc(s_place, 1)

            def route_places_t():
                dve.wait_ge(s_placeT, 1)
                V.tensor_copy(placeT[:, 0:4], ps[:, 6, :].bitcast(F16).rearrange("p (r t) -> p r t", t=TOK))\
                    .then_inc(s_placed, 1)
                V.tensor_copy(placeT[:, 4], ps[:, 7, 0:TOK // 2].bitcast(F16)).then_inc(s_placed, 1)

            def rows_lo():
                dve.wait_ge(s_xnh, 1)
                V.tensor_tensor(xnl[:], acc[:], xnh[:], ALU.subtract).then_inc(s_xnl, 1)

            routing = {(0, 0): route_top, (0, 1): route_weights, (0, 2): rows_lo, (0, 5): route_order,
                       (0, 6): route_mine, (1, 4): route_places, (2, 4): route_places_t}

            def product(i, slot):
                dve.wait_ge(s_sil, i + 1)
                need(dve, s_hl, i - 1)
                V.tensor_tensor(hf[:, slot % 2], sil[:, slot % 2], ps[:, slot, TOK:2 * TOK], ALU.mult)\
                    .then_inc(s_h, 1)

            def hidden_lo(i, slot):
                dve.wait_ge(s_hh, i + 1)
                V.tensor_tensor(hl[:, slot], hf[:, slot % 2], hh[:, slot], ALU.subtract).then_inc(s_hl, 1)

            def combine(e):
                for b in range(TB):
                    if e >= ND:
                        dve.wait_ge(s_cs, TB * (e - ND) + b + 1)
                        bank = 7 - b
                    elif b == 0:
                        dve.wait_ge(s_Y, e + 1)
                        bank = 4
                    else:
                        dve.wait_ge(s_h2, HB * e + HB)
                        bank = 5
                    need(dve, s_macc, TB * e)
                    V.scalar_tensor_tensor(macc[:, b], ps[:, bank, :], comb[:, b, e:e + 1], macc[:, b],
                                           ALU.mult, ALU.add).then_inc(s_macc, 1)

            def expert(e, par):
                for b in range(HB):
                    i = HB * e + b
                    if e > 0 and b == 2:
                        combine(e - 1)
                    product(i, b % 4)
                    if (e, b) in routing:
                        routing[e, b]()
                    if b >= 2:
                        split_lo(e + 1, 1 - par, b - 2)
                    hidden_lo(i, b % 4)

            for e in range(ND):
                expert(e, e % 2)

            def gathered_lo(r, bank):
                dve.wait_ge(s_xg, r + 1)
                V.tensor_copy(xgl[:], ps[:, bank, :].rearrange("p (c t) -> p c t", t=P)).then_inc(s_xgl, 1)

            def gathered(r):
                e, par = ND + r, (ND + r) % 2

                def half(h):
                    dve.wait_ge(s_csil, 2 * r + h + 1)
                    need(dve, s_cT, 2 * (r - 1) + h + 1)
                    V.tensor_tensor(ch[:, h], csil[:, h], ps[:, 2 * h + 1, :], ALU.mult).then_inc(s_cp, 1)

                def hidden(h):
                    dve.wait_ge(s_chh, 2 * r + h + 1)
                    V.tensor_tensor(chl[:, 4 * h:4 * h + 4], ps[:, 4 + h, :].rearrange("p (c t) -> p c t", t=P),
                                    chh[:, 4 * h:4 * h + 4], ALU.subtract).then_inc(s_chl, 1)

                def split(k):
                    if r < NC - 1:
                        split_lo(e + 1, 1 - par, k)

                if r == 0:
                    combine(ND - 1)
                split(0)
                split(1)
                half(0)
                if r > 0:
                    combine(e - 1)
                split(2)
                hidden(0)
                split(3)
                half(1)
                split(4)
                hidden(1)
                if r < NC - 1:
                    gathered_lo(r + 1, 7)
                split(5)
                dve.wait_ge(s_yh, r + 1)
                V.scalar_tensor_tensor(yl[:], ps[:, 6, :], 1.0 / WSC, yh[:], ALU.mult, ALU.subtract).then_inc(s_yl, 1)

            gathered_lo(0, 7)
            for r in range(NC):
                gathered(r)
            combine(NX - 1)

        @block.tensor
        def _(pe):
            mm = nc.tensor.matmul

            def transpose_rows(bank, src):
                for c in range(DC):
                    for b in range(TB):
                        last = nc.tensor.transpose(cols(bank)[:, c, b * P:(b + 1) * P], src[:, b, c * P:(c + 1) * P],
                                                   ident[:])
                last.then_inc(s_pe, 1)

            def project_t(bank, w, src):
                for o in range(DC):
                    for c in range(DC):
                        last = mm(cols(bank)[:, o], wts[:, w, c, o * P:(o + 1) * P], src[:, c],
                                  start=(c == 0), stop=(c == DC - 1))
                last.then_inc(s_pe, 1)

            def project(bank, w, src, first=True, final=True):
                for b in range(TB):
                    for c in range(DC):
                        last = mm(ps[:, bank + b, :], src(c, b), wts[:, w, c, :],
                                  start=(first and c == 0), stop=(final and c == DC - 1))
                last.then_inc(s_pe, 1)

            def scores(n, par, b):
                for c in range(DC):
                    for q, k in ((qTh, cTh), (qTh, cTl), (qTl, cTh)):
                        for h in range(2):
                            last = mm(psS[:, 2 * b + h, 0:HALF], q[:, c, b * P:(b + 1) * P],
                                      k[:, par, c, h * HALF:(h + 1) * HALF],
                                      start=(c == 0 and q is qTh and k is cTh), stop=(c == DC - 1 and q is qTl))
                last.then_inc(s_S, 1)

            def transposes(g, j):
                a, b = PAIR_TILES[j]
                for t in range(a, b):
                    for q in range(TB):
                        last = nc.tensor.transpose(psT[:, j % 2, (t - a) * TOK + q * P:(t - a) * TOK + (q + 1) * P],
                                                   prob[:, q, t * P:(t + 1) * P], ident[:])
                last.then_inc(s_T, 1)

            pe.wait_ge(s_ident, 2)
            pe.wait_ge(s_ln, 6)
            transpose_rows(4, xn)
            pe.wait_ge(s_ev, 1)
            pe.wait_ge(s_wqk, 32)
            project_t(6, 0, xnT)
            pe.wait_ge(s_ev, 2)
            project_t(4, 1, qpT)
            pe.wait_ge(s_qh, 1)
            pe.wait_ge(s_ql, 1)
            pe.wait_ge(s_hiT, 4)
            pe.wait_ge(s_loT, 4)
            for b in range(TB):
                scores(0, 0, b)

            def step(g, par, more=True):
                pe.wait_ge(s_exp, 2 * g + 2)
                need(pe, s_ptl, PAIRS * g)
                for j in (0, 1):
                    transposes(g, j)
                if more:
                    pe.wait_ge(s_hiT, 4 * g + 8)
                    pe.wait_ge(s_loT, 4 * g + 8)
                    scores(g + 1, 1 - par, 0)
                for j in (2, 3):
                    pe.wait_ge(s_ptl, PAIRS * g + j - 1)
                    transposes(g, j)
                if more:
                    scores(g + 1, 1 - par, 1)
                pe.wait_ge(s_hiN, 4 * g + 4)
                pe.wait_ge(s_loN, 4 * g + 4)
                need(pe, s_acc, 2 * g)
                for b in range(TB):
                    for t in range(KT):
                        if b == 0 and t % 2 == 0:
                            pe.wait_ge(s_pth, PAIRS * g + t // 2 + 1)
                            pe.wait_ge(s_ptl, PAIRS * g + t // 2 + 1)
                        for p, k in ((pTh, cNh), (pTh, cNl), (pTl, cNh)):
                            last = mm(psO[:, b, :], p[:, t, b * P:(b + 1) * P], k[:, par, t],
                                      start=(t == 0 and p is pTh and k is cNh), stop=(t == KT - 1 and p is pTl))
                    last.then_inc(s_PV, 1)

            step(0, 0)
            with pe.Fori(0, (NG - 4) // 2) as i:
                step(2 * i + 1, 1)
                step(2 * i + 2, 0)
            step(NG - 3, 1)
            step(NG - 2, 0)
            step(NG - 1, 1, more=False)

            pe.wait_ge(s_ev, 3)
            transpose_rows(0, acc)
            pe.wait_ge(s_ev, 4)
            pe.wait_ge(s_wvo, 32)
            project_t(2, 0, t1)
            pe.wait_ge(s_zt, DC)
            project(4, 1, lambda c, b: t2[:, c, b * P:(b + 1) * P])
            pe.wait_ge(s_ln, 12)
            transpose_rows(0, acc)
            pe.wait_ge(s_ev, 5)
            pe.wait_ge(s_w12, 32)
            for b in range(TB):
                for c in range(DC):
                    last = mm(ps[:, 2 + b, :], xpad[:, c, TAPS - 1 + b * P:TAPS - 1 + (b + 1) * P], wts[:, 2, c, :],
                              start=(c == 0), stop=False)
            last.then_inc(s_pe, 1)
            for c in range(DC):
                pe.wait_ge(s_zero, DC * (TAPS - 2) + c + 1)
                for b in range(TB):
                    last = mm(ps[:, 2 + b, :], t1[:, c, b * P:(b + 1) * P], wts[:, 3, c, :],
                              start=False, stop=(c == DC - 1))
            last.then_inc(s_pe, 1)
            pe.wait_ge(s_ln, 18)
            transpose_rows(0, acc)
            pe.wait_ge(s_ev, 6)
            for b in range(TB):
                for c in range(DC):
                    last = mm(ps[:, 6, NE * b:NE * b + NE], t2[:, c, b * P:(b + 1) * P], router_sb[:, c],
                              start=(c == 0), stop=(c == DC - 1))
            last.then_inc(s_pe, 1)
            pe.wait_ge(s_qh, 2)
            pe.wait_ge(s_ql, 2)

            def first(e, par, b):
                i = HB * e + b
                if b == 0:
                    pe.wait_ge(s_whi, PIECES * e + 4)
                    pe.wait_ge(s_wlo, PIECES * e + 4)
                need(pe, s_h, i - 3)
                for m in range(2):
                    for c in range(DC):
                        for w, xt in ((wh, xTh), (wh, xTl), (wl, xTh)):
                            last = mm(ps[:, b % 4, m * TOK:(m + 1) * TOK], w13(w, par, m)[:, c, b * P:(b + 1) * P],
                                      xt[:, c], start=(c == 0 and w is wh and xt is xTh),
                                      stop=(c == DC - 1 and w is wl))
                last.then_inc(s_H, 1)

            def second(e, par, b):
                i = HB * e + b
                if b == 0:
                    pe.wait_ge(s_whi, PIECES * e + PIECES)
                    pe.wait_ge(s_wlo, PIECES * e + PIECES)
                    need(pe, s_macc, TB * e)
                pe.wait_ge(s_hh, i + 1)
                pe.wait_ge(s_hl, i + 1)
                for q in range(TB):
                    for h, w in ((hh, wh), (hh, wl), (hl, wh)):
                        last = mm(ps[:, 4 + q, :], h[:, b % 4, q * P:(q + 1) * P], w2(w, par)[:, b],
                                  start=(b == 0 and h is hh and w is wh), stop=(b == HB - 1 and h is hl))
                    if b == HB - 1 and q == 0:
                        last.then_inc(s_Y, 1)
                last.then_inc(s_h2, 1)

            def count_rows():
                pe.wait_ge(s_chosen, 1)
                pe.wait_ge(s_iota, 6)
                for b in range(TB):
                    last = mm(ps[:, 6, 0:NE], ones16[:], chosen16[:, b], start=(b == 0), stop=(b == TB - 1))
                last.then_inc(s_load, 1)

            def number_rows():
                pe.wait_ge(s_mine, 1)
                mm(ps[:, 6, 0:NC], before16[:], mine16[:, 0], start=True, stop=True)
                mm(ps[:, 6, NC:2 * NC], ones16[:], mine16[:, 0], start=True, stop=False)
                mm(ps[:, 6, NC:2 * NC], before16[:], mine16[:, 1], start=False, stop=True).then_inc(s_slot, 1)

            def turn_places():
                pe.wait_ge(s_place, 1)
                for r in range(NC):
                    for b in range(TB):
                        o = ((r % 4) * TB + b) * P
                        last = nc.tensor.transpose(ps[:, 6 + r // 4, :].bitcast(F16)[:, o:o + P], place[:, r, b],
                                                   ident16[:])
                last.then_inc(s_placeT, 1)

            def gather(r, bank_h, bank_l):
                for bank, rows in ((bank_h, xnh), (bank_l, xnl)):
                    for c in range(DC):
                        for b in range(TB):
                            last = mm(ps[:, bank, c * P:(c + 1) * P], rows[:, b, c * P:(c + 1) * P], place[:, r, b],
                                      start=(b == 0), stop=(b == TB - 1))
                last.then_inc(s_xg, 1)

            def first_gather():
                pe.wait_ge(s_xnl, 1)
                pe.wait_ge(s_placed, 2)
                gather(0, 6, 7)

            routing = {(0, 4): count_rows, (1, 2): number_rows, (2, 2): turn_places, (ND - 1, 5): first_gather}

            def expert(e, par):
                for b in range(2, HB + 2):
                    if b < HB:
                        first(e, par, b)
                    elif e < ND - 1:
                        first(e + 1, 1 - par, b - HB)
                    if (e, b) in routing:
                        routing[e, b]()
                    second(e, par, b - 2)

            def scatter(r):
                pe.wait_ge(s_yh, r + 1)
                pe.wait_ge(s_yl, r + 1)
                for b in range(TB):
                    mm(ps[:, 7 - b, :], placeT[:, r, b * P:(b + 1) * P], yh[:], start=True, stop=False)
                    mm(ps[:, 7 - b, :], placeT[:, r, b * P:(b + 1) * P], yl[:], start=False, stop=True)\
                        .then_inc(s_cs, 1)

            def gathered(r):
                e, par = ND + r, (ND + r) % 2

                def matrix(m, h):
                    for c in range(DC):
                        for w, xt in ((wh, xgh), (wh, xgl), (wl, xgh)):
                            last = mm(ps[:, 2 * h + m, :], xt[:, c], w13(w, par, m)[:, c, h * HH:(h + 1) * HH],
                                      start=(c == 0 and w is wh and xt is xgh), stop=(c == DC - 1 and w is wl))
                    return last

                def turn(h):
                    pe.wait_ge(s_cp, 2 * r + h + 1)
                    for c in range(4):
                        last = nc.tensor.transpose(ps[:, 4 + h, c * P:(c + 1) * P], ch[:, h, c * P:(c + 1) * P],
                                                   ident[:])
                    last.then_inc(s_cT, 1)

                def output(h):
                    pe.wait_ge(s_chh, 2 * r + h + 1)
                    pe.wait_ge(s_chl, 2 * r + h + 1)
                    for b in range(4 * h, 4 * h + 4):
                        for hd, w in ((chh, wh), (chh, wl), (chl, wh)):
                            last = mm(ps[:, 6, :], hd[:, b], w2(w, par)[:, b],
                                      start=(b == 0 and hd is chh and w is wh), stop=(b == HB - 1 and hd is chl))
                    return last

                pe.wait_ge(s_xgh, r + 1)
                pe.wait_ge(s_xgl, r + 1)
                pe.wait_ge(s_whi, PIECES * e + 4)
                pe.wait_ge(s_wlo, PIECES * e + 4)
                need(pe, s_cp, 2 * r - 1)
                if r == 0:
                    pe.wait_ge(s_h, HB * ND)
                matrix(0, 0)
                matrix(1, 0).then_inc(s_c1, 1)
                if r > 0:
                    scatter(r - 1)
                    pe.wait_ge(s_cp, 2 * r)
                matrix(0, 1)
                if r == 0:
                    pe.wait_ge(s_macc, TB * ND)
                turn(0)
                matrix(1, 1).then_inc(s_c1, 1)
                pe.wait_ge(s_whi, PIECES * e + PIECES)
                pe.wait_ge(s_wlo, PIECES * e + PIECES)
                pe.wait_ge(s_macc, TB * e)
                output(0)
                turn(1)
                if r < NC - 1:
                    gather(r + 1, 4, 7)
                output(1).then_inc(s_cY, 1)

            first(0, 0, 0)
            first(0, 0, 1)
            for e in range(ND):
                expert(e, e % 2)
            for r in range(NC):
                gathered(r)
            scatter(NC - 1)


def kernel(**inputs):
    import numpy as np
    import concourse.bacc as bacc
    from concourse.bass_utils import run_bass_kernel_spmd

    a = {name: np.asarray(v) for name, v in inputs.items()}

    def chunks(w):
        return w.reshape(DC, P, -1).transpose(1, 0, 2)

    def piece(w):
        return w.reshape(-1, P, w.shape[1]).transpose(1, 0, 2).reshape(P, -1)

    f = "L0_ffn_"
    experts = [(a[f + "sw1"][i], a[f + "sw3"][i], a[f + "sw2"][i]) for i in range(NS)]
    experts += [(a[f + "w1"][i], a[f + "w3"][i], a[f + "w2"][i]) for i in range(NE)]
    ctx = a["ctx_1024"].reshape(NG, P, KT, DC, P)
    arrays = {
        "x": a["x"],
        "ctx_nat": ctx.reshape(NG, P, KT, D),
        "ctx_t": ctx.transpose(0, 4, 3, 2, 1).reshape(NG, P, DC, GK),
        "wmats": np.stack([chunks(a["L0_xattn_Wq"].T), chunks(a["L0_xattn_Wk"]), chunks(a["L0_xattn_Wv"].T),
                           chunks(a["L0_xattn_Wo"].T), chunks(a["L0_attn_W1"]), chunks(a["L0_attn_W2"])]),
        "bq": a["L0_xattn_bq"].reshape(DC, P).T,
        "bv": a["L0_xattn_bv"].reshape(DC, P).T,
        "bo": a["L0_xattn_bo"],
        "bias": a["L0_attn_bias"],
        "table": chunks(a["L0_attn_embeddings_table"].T),
        "router": chunks(a[f + "router_w"].T),
        "ebias": a[f + "expert_bias"],
        "wexp": np.stack([np.concatenate([piece(w1.T), piece(w3.T), piece(w2.T)], axis=1) for w1, w3, w2 in experts]),
    }
    nc = bacc.Bacc("TRN2", target_bir_lowering=False, num_devices=1)
    args, ins = [], {}
    for name, v in arrays.items():
        ins[f"{name}_dram"] = np.ascontiguousarray(v)
        args.append(nc.dram_tensor(f"{name}_dram", v.shape, mybir.dt.from_np(v.dtype), kind="ExternalInput").ap())
    args.append(nc.dram_tensor("out_dram", a["x"].shape, F32, kind="ExternalOutput").ap())
    perceiver_kernel(nc, *args)
    r = run_bass_kernel_spmd(nc, [ins], core_ids=[0])
    return r.results[0]["out_dram"]
```

```python
from contextlib import ExitStack
import math

import concourse.bass as bass
from concourse import mybir

P = 128
F32 = mybir.dt.float32
F16 = mybir.dt.float16
U32 = mybir.dt.uint32
ALU = mybir.AluOpType
ACT = mybir.ActivationFunctionType
AX = mybir.AxisListType

D = 512
DC = D // P
TOK = 256
TB = TOK // P
KEYS = 25088
KT = 7
GK = KT * P
NG = KEYS // GK
HALF = GK // 2
PAIRS = 4
TAPS = 21
SPLIT_TAP = 6
PE_TAPS = [(3, j) for j in range(1, TAPS)] + [(2, j) for j in range(SPLIT_TAP, TAPS)]
NE = 8
NS = 2
NX = NS + NE
ND = NS + 3
NC = NX - ND
HID = 1024
HB = HID // P
HH = HID // 2
PIECE = 2048
PIECES = 3 * 4096 // PIECE
SC = 1.0 / math.sqrt(D)
LN_P = 12 * math.log(2.0)
WSC = 64.0
EPS = 1e-5


def need(eng, sem, count):
    if not (isinstance(count, int) and count <= 0):
        eng.wait_ge(sem, count)


def perceiver_kernel(nc, x, ctx_nat, ctx_t, wmats, bq, bv, bo, bias, table, router, ebias, wexp, out):
    with ExitStack() as keep:
        def sb(name, shape, dt, stack=keep):
            return stack.enter_context(nc.sbuf_tensor(name, shape, dt))

        def sem(name):
            return keep.enter_context(nc.semaphore(name))

        ident = sb("ident", [P, P], F32)
        mid_rows = ExitStack()
        x1 = sb("x1", [P, TB, D], F32, mid_rows)
        bo_b = sb("bo_b", [P, D], F32, mid_rows)
        bias_b = sb("bias_b", [P, D], F32, mid_rows)
        mid_rows.close()
        wraw5 = sb("wraw5", [P, PIECE], F32)
        acc = sb("acc", [P, TB, D], F32)
        ebias_b = sb("ebias_b", [P, NE], F32)
        bq_sb = sb("bq_sb", [P, DC], F32)
        bv_sb = sb("bv_sb", [P, DC], F32)
        table_sb = sb("table_sb", [P, DC, TAPS], F32)
        router_sb = sb("router_sb", [P, DC, NE], F32)
        stats = sb("stats", [P, TB, 6], F32)
        mv = sb("mv", [P, TB, 2], F32)
        var_e = sb("var_e", [P, TB], F32)
        std = sb("std", [P, TB], F32)
        rstd = sb("rstd", [P, TB], F32)
        mx = sb("mx", [P, 2, TB], F32)
        cm = sb("cm", [P, TB], F32)
        nb = sb("nb", [P, 2, TB], F32)
        dm = sb("dm", [P, 2, TB], F32)
        alpha = sb("alpha", [P, 2, TB], F32)
        rs = sb("rs", [P, 2, TB], F32)
        den = sb("den", [P, TB], F32)
        rden = sb("rden", [P, TB], F32)
        iota8 = sb("iota8", [P, NE], F32)
        iota_s = sb("iota_s", [P, P], F32)
        ones16 = sb("ones16", [P, P], F16)
        before16 = sb("before16", [P, P], F16)
        ident16 = sb("ident16", [P, P], F16)
        logits = sb("logits", [P, TB, NE], F32)
        top = sb("top", [P, TB, 8], F32)
        topi = sb("topi", [P, TB, 8], U32)
        topf = sb("topf", [P, TB, 8], F32)
        pr = sb("pr", [P, TB, 4], F32)
        sel = sb("sel", [P, TB, 2, NE], F32)
        cbase = sb("cbase", [P, TB, NE], F32)
        comb = sb("comb", [P, TB, NX], F32)
        second16 = sb("second16", [P, TB, NE], F16)
        chosen16 = sb("chosen16", [P, TB, NE], F16)
        load = sb("load", [P, NE], F32)
        load_top = sb("load_top", [P, NE], F32)
        order = sb("order", [P, NE], U32)
        order_f = sb("order_f", [P, NE], F32)
        picked = sb("picked", [P, TB, NE, NE], F32)
        mine = sb("mine", [P, TB, NC], F32)
        mine16 = sb("mine16", [P, TB, NC], F16)
        slot = sb("slot", [P, TB, NC], F32)

        old = ExitStack()
        wts = sb("wts", [P, 4, DC, D], F32, old)
        old.close()
        place = sb("place", [P, NC, TB, P], F16)
        placeT = sb("placeT", [P, NC, TOK], F16)
        xnh = sb("xnh", [P, TB, D], F16)
        xnl = sb("xnl", [P, TB, D], F16)
        xgh = sb("xgh", [P, DC, P], F16)
        xgl = sb("xgl", [P, DC, P], F16)
        csil = sb("csil", [P, 2, HH], F32)
        ch = sb("ch", [P, 2, HH], F32)
        chh = sb("chh", [P, HB, P], F16)
        chl = sb("chl", [P, HB, P], F16)
        yh = sb("yh", [P, D], F16)
        yl = sb("yl", [P, D], F16)
        used = 2 * (NC * TB * P + NC * TOK + 2 * TB * D + 2 * DC * P + 2 * HB * P + 2 * D) + 4 * 4 * HH
        rest = sb("rest", [P, (4 * DC * D * 4 - used) // 4], F32)

        att = ExitStack()
        rawT = sb("rawT", [P, 2, DC, GK], F32, att)
        rawN = sb("rawN", [P, 2, KT, D], F32, att)
        cTh = sb("cTh", [P, 2, DC, GK], F16, att)
        cTl = sb("cTl", [P, 2, DC, GK], F16, att)
        cNh = sb("cNh", [P, 2, KT, D], F16, att)
        cNl = sb("cNl", [P, 2, KT, D], F16, att)
        prob = sb("prob", [P, TB, GK], F32, att)
        pTh = sb("pTh", [P, KT, TOK], F16, att)
        pTl = sb("pTl", [P, KT, TOK], F16, att)
        qTh = sb("qTh", [P, DC, TOK], F16, att)
        qTl = sb("qTl", [P, DC, TOK], F16, att)
        land = sb("land", [P, DC, D], F32, att)
        dtap = sb("dtap", [P, P], F32, att)
        diagh = sb("diagh", [P, len(PE_TAPS), P], F16, att)
        diagl = sb("diagl", [P, len(PE_TAPS), P], F16, att)
        att.close()
        wraw = sb("wraw", [P, 4, PIECE], F32)
        wh = sb("wh", [P, 2, PIECES, PIECE], F16)
        memory = ExitStack()
        t1 = sb("t1", [P, DC, TOK], F32, memory)
        xpad = sb("xpad", [P, DC, TAPS - 1 + TOK], F32, memory)
        memory.close()
        wraw4 = sb("wraw4", [P, PIECE], F32)
        memory_end = sb("memory_end", [P, DC * (TAPS - 1 + 2 * TOK) - PIECE], F32)
        t2 = sb("t2", [P, DC, TOK], F32)
        macc = sb("macc", [P, TB, D], F32)
        xTh = sb("xTh", [P, DC, TOK], F16)
        xTl = sb("xTl", [P, DC, TOK], F16)
        mid = ExitStack()
        t1h = sb("t1h", [P, DC, TOK], F16, mid)
        t1l = sb("t1l", [P, DC, TOK], F16, mid)
        xph = sb("xph", [P, DC, TAPS - 1 + TOK], F16, mid)
        xpl = sb("xpl", [P, DC, TAPS - 1 + TOK], F16, mid)
        mid.close()
        sil = sb("sil", [P, 2, TOK], F32)
        hf = sb("hf", [P, 2, TOK], F32)
        hh = sb("hh", [P, 4, TOK], F16)
        hl = sb("hl", [P, 4, TOK], F16)
        mid_end = sb("mid_end", [P, 2 * (TAPS - 1) * DC // 2], F32)
        wl = sb("wl", [P, 2, PIECES, PIECE], F16)

        xn = prob[:, :, 0:D]
        x_sb = rawN[:, 1, 4:6, :]
        xnT = rawN[:, 1, 0:2, :].rearrange("p a (b t) -> p (a b) t", t=TOK)
        qpT = rawN[:, 1, 2:4, :].rearrange("p a (b t) -> p (a b) t", t=TOK)

        ps = keep.enter_context(nc.psum_tensor("ps", [P, 8, 512], F32))
        psS = ps[:, 0:4, :]
        psT = ps[:, 4:6, :]
        psO = ps[:, 6:8, :]

        def cols(bank):
            return ps[:, bank:bank + 2, :].rearrange("p a (b t) -> p (a b) t", t=TOK)

        def square(m):
            parts = wts[:, m].rearrange("p c n -> p (c n)").bitcast(F16).rearrange("p (s c n) -> p s c n", s=2, n=D)
            return parts[:, 0], parts[:, 1]

        landing = [wraw[:, k] for k in range(4)] + [wraw4[:], wraw5[:]]

        def w13(t, par, m):
            return t[:, par, 2 * m:2 * m + 2, :].rearrange("p a (c h) -> p (a c) h", h=HID)

        def w2(t, par):
            return t[:, par, 4:6, :].rearrange("p a (c n) -> p (a c) n", n=D)

        s_x = [sem(f"s_x{b}") for b in range(TB)]
        s_wq = sem("s_wq")
        s_wk = sem("s_wk")
        s_small = sem("s_small")
        s_land = sem("s_land")
        s_sqh = sem("s_sqh")
        s_sql = sem("s_sql")
        s_zh = sem("s_zh")
        s_zl = sem("s_zl")
        s_xph = sem("s_xph")
        s_xpl = sem("s_xpl")
        s_x3 = sem("s_x3")
        s_x3d = sem("s_x3d")
        s_hth = sem("s_hth")
        s_htl = sem("s_htl")
        s_ht2 = sem("s_ht2")
        s_rawT = [sem(f"s_rawT{i}") for i in range(2)]
        s_rawN = [sem(f"s_rawN{i}") for i in range(2)]
        s_ident = sem("s_ident")
        s_iota = sem("s_iota")
        s_init = sem("s_init")
        s_dve = sem("s_dve")
        s_stats = sem("s_stats")
        s_mean = sem("s_mean")
        s_var = sem("s_var")
        s_std = sem("s_std")
        s_norm = sem("s_norm")
        s_pe = sem("s_pe")
        s_ev = sem("s_ev")
        s_eva = sem("s_eva")
        s_res = sem("s_res")
        s_diag = sem("s_diag")
        s_xh = sem("s_xh")
        s_xl = sem("s_xl")
        s_qh = sem("s_qh")
        s_ql = sem("s_ql")
        s_hiT = sem("s_hiT")
        s_loT = sem("s_loT")
        s_hiN = sem("s_hiN")
        s_loN = sem("s_loN")
        s_S = sem("s_S")
        s_cm = sem("s_cm")
        s_mx = sem("s_mx")
        s_ref = sem("s_ref")
        s_ref0 = sem("s_ref0")
        s_alpha = sem("s_alpha")
        s_exp = sem("s_exp")
        s_T = sem("s_T")
        s_pth = sem("s_pth")
        s_ptl = sem("s_ptl")
        s_PV = sem("s_PV")
        s_acc = sem("s_acc")
        s_den = sem("s_den")
        s_zero = sem("s_zero")
        s_gap = sem("s_gap")
        s_gexp = sem("s_gexp")
        s_xnh = sem("s_xnh")
        s_xnl = sem("s_xnl")
        s_chosen = sem("s_chosen")
        s_load = sem("s_load")
        s_order = sem("s_order")
        s_mine = sem("s_mine")
        s_slot = sem("s_slot")
        s_place = sem("s_place")
        s_placeT = sem("s_placeT")
        s_placed = sem("s_placed")
        s_xg = sem("s_xg")
        s_xgh = sem("s_xgh")
        s_xgl = sem("s_xgl")
        s_c1 = sem("s_c1")
        s_csil = sem("s_csil")
        s_cp = sem("s_cp")
        s_cT = sem("s_cT")
        s_chh = sem("s_chh")
        s_chl = sem("s_chl")
        s_cY = sem("s_cY")
        s_yh = sem("s_yh")
        s_yl = sem("s_yl")
        s_cs = sem("s_cs")
        s_wraw = [sem(f"s_wraw{i}") for i in range(PIECES)]
        s_whi = sem("s_whi")
        s_wlo = sem("s_wlo")
        s_scaled = sem("s_scaled")
        s_H = sem("s_H")
        s_sil = sem("s_sil")
        s_h = sem("s_h")
        s_hh = sem("s_hh")
        s_hl = sem("s_hl")
        s_h2 = sem("s_h2")
        s_Y = sem("s_Y")
        s_macc = sem("s_macc")
        s_out = sem("s_out")

        PAIR_TILES = [(0, 2), (2, 4), (4, 6), (6, 7)]
        tok_view = lambda a: a.rearrange("o (b p) d -> p (o b) d", p=P)

        H_DONE = 1 + 2 * (TAPS - 1) + SPLIT_TAP

        block = keep.enter_context(nc.Block())

        @block.sync
        def _(sp):
            for b in range(TB):
                sp.dma_start(x_sb[:, b], tok_view(x)[:, b]).then_inc(s_x[b], 16)
            sp.dma_start(wts[:, 0], wmats[0]).then_inc(s_wq, 16)
            sp.dma_start(wts[:, 1], wmats[1]).then_inc(s_wk, 16)
            small = [(bq_sb[:], bq), (bv_sb[:], bv), (table_sb[:], table), (router_sb[:], router),
                     (bo_b[:], bo.partition_broadcast(P)), (bias_b[:], bias.partition_broadcast(P)),
                     (ebias_b[:], ebias.partition_broadcast(P))]
            for dst, src in small:
                sp.dma_start(dst, src).then_inc(s_small, 16)

            def load_t(g, slot):
                sp.dma_start(rawT[:, slot], ctx_t[g]).then_inc(s_rawT[slot], 16)

            def load_n(g, slot):
                sp.dma_start(rawN[:, slot], ctx_nat[g]).then_inc(s_rawN[slot], 16)

            def split_t(count):
                sp.wait_ge(s_hiT, 4 * count)
                sp.wait_ge(s_loT, 4 * count)

            def split_n(count):
                sp.wait_ge(s_hiN, 4 * count)
                sp.wait_ge(s_loN, 4 * count)

            load_t(0, 0)
            load_t(1, 1)
            load_n(0, 0)
            split_t(1)
            load_t(2, 0)
            sp.wait_ge(s_qh, 2)
            sp.wait_ge(s_ql, 2)
            sp.wait_ge(s_res, TB)
            load_n(1, 1)
            split_t(2)
            load_t(3, 1)
            split_n(1)
            load_n(2, 0)

            def load_square(m):
                if m > 0:
                    sp.wait_ge(s_sql, m)
                sp.dma_start(land[:], wmats[2 + m]).then_inc(s_land, 16)

            load_square(0)

            def pair(i):
                split_t(2 * i - 1)
                load_t(2 * i, 0)
                split_n(2 * i - 2)
                load_n(2 * i - 1, 1)
                split_t(2 * i)
                load_t(2 * i + 1, 1)
                split_n(2 * i - 1)
                load_n(2 * i, 0)

            for i in (2, 3, 4):
                pair(i)
                load_square(i - 1)
            with sp.Fori(5, NG // 2) as i:
                pair(i)
            split_n(NG - 2)
            load_n(NG - 1, 1)

            def load_piece(expert, k):
                sp.dma_start(landing[k], wexp[expert, :, k * PIECE:(k + 1) * PIECE]).then_inc(s_wraw[k], 16)

            split_t(NG)
            split_n(NG)
            for k in range(4):
                load_piece(0, k)
            sp.wait_ge(s_xpl, 2)
            sp.wait_ge(s_htl, 3)
            sp.wait_ge(s_ht2, 1)
            load_piece(0, 4)
            sp.wait_ge(s_norm, 3 * TB)
            load_piece(0, 5)
            for k in range(PIECES):
                sp.wait_ge(s_wlo, k + 1)
                load_piece(1, k)
            sp.wait_ge(s_order, 1)
            with sp.Fori(NS // 2, NX // 2) as i:
                for par in range(2):
                    e = 2 * i + par
                    routed = sp.value_load(order[0:1, bass.ds(e - NS, 1)], min_val=0, max_val=NE - 1)
                    for k in range(PIECES):
                        sp.wait_ge(s_wlo, PIECES * e - PIECES + k + 1)
                        load_piece(routed + NS, k)
            for b in range(TB):
                sp.wait_ge(s_macc, TB * NX - TB + b + 1)
                sp.dma_start(tok_view(out)[:, b, :], macc[:, b, :]).then_inc(s_out, 16)
            sp.wait_ge(s_out, 16 * TB)

        @block.gpsimd
        def _(pool):
            nc.gpsimd.memset(ident[:], 0.0).then_inc(s_ident, 1)
            pool.wait_ge(s_ident, 1)
            nc.gpsimd.affine_select(out=ident[:], in_=ident[:], compare_op=ALU.not_equal, fill=1.0, base=0,
                                    pattern=[[-1, P]], channel_multiplier=1).then_inc(s_ident, 1)
            nc.gpsimd.iota(iota8[:], pattern=[[1, NE]], base=0, channel_multiplier=0,
                           allow_small_or_imprecise_dtypes=True).then_inc(s_iota, 1)
            nc.gpsimd.memset(comb[:, :, 0:NS], 1.0 / (WSC * WSC)).then_inc(s_iota, 1)
            nc.gpsimd.iota(iota_s[:], pattern=[[1, P]], base=0, channel_multiplier=0,
                           allow_small_or_imprecise_dtypes=True).then_inc(s_iota, 1)
            nc.gpsimd.memset(ones16[:], 1.0).then_inc(s_iota, 1)
            pool.wait_ge(s_iota, 4)
            nc.gpsimd.affine_select(out=before16[:], in_=ones16[:], compare_op=ALU.is_gt, fill=0.0, base=0,
                                    pattern=[[1, P]], channel_multiplier=-1).then_inc(s_iota, 1)
            pool.wait_ge(s_ident, 2)
            nc.gpsimd.tensor_copy(ident16[:], ident[:]).then_inc(s_iota, 1)
            for b in range(TB):
                pool.wait_ge(s_x[b], 16)
            pool.wait_ge(s_small, 16 * 7)
            for b in range(TB):
                nc.gpsimd.tensor_tensor(x1[:, b], x_sb[:, b], bo_b[:], ALU.add).then_inc(s_res, 1)
            for n, (c, j) in enumerate(PE_TAPS):
                if n > 0:
                    pool.wait_ge(s_diag, 3 * n)
                nc.gpsimd.tensor_scalar(dtap[:], ident[:], table_sb[:, c, j:j + 1], WSC, ALU.mult, ALU.mult)\
                    .then_inc(s_diag, 1)
                pool.wait_ge(s_diag, 3 * n + 1)
                nc.gpsimd.tensor_copy(diagh[:, n], dtap[:]).then_inc(s_diag, 1)
                pool.wait_ge(s_diag, 3 * n + 2)
                nc.gpsimd.tensor_tensor(diagl[:, n], dtap[:], diagh[:, n], ALU.subtract).then_inc(s_diag, 1)
            for h in (1, 0):
                pool.wait_ge(s_xph, 2 - h)
                pool.wait_ge(s_x3, 1)
                nc.gpsimd.tensor_tensor(xpl[:, 2 * h:2 * h + 2, TAPS - 1:], xpad[:, 2 * h:2 * h + 2, TAPS - 1:],
                                        xph[:, 2 * h:2 * h + 2, TAPS - 1:], ALU.subtract).then_inc(s_xpl, 1)
            for b in range(TB):
                pool.wait_ge(s_norm, 2 * TB)
                nc.gpsimd.tensor_tensor(x1[:, b], x1[:, b], bias_b[:], ALU.add).then_inc(s_res, 1)
            pool.wait_ge(s_whi, 4)
            pool.wait_ge(s_wlo, 3)
            nc.gpsimd.tensor_scalar(landing[3], landing[3], WSC, None, ALU.mult).then_inc(s_scaled, 1)
            pool.wait_ge(s_scaled, 1)
            nc.gpsimd.tensor_tensor(wl[:, 0, 3], landing[3], wh[:, 0, 3], ALU.subtract).then_inc(s_wlo, 1)
            for n, c in enumerate((0, 1, 3)):
                pool.wait_ge(s_hth, n + 1)
                nc.gpsimd.tensor_tensor(t1l[:, c], t1[:, c], t1h[:, c], ALU.subtract).then_inc(s_htl, 1)

        @block.scalar
        def _(act):
            def root(m):
                act.wait_ge(s_var, m + 1)
                nc.scalar.activation(std[:, m % TB:m % TB + 1], var_e[:, m % TB:m % TB + 1], ACT.Sqrt)\
                    .then_inc(s_std, 1)

            def hi_t(g, par, c):
                nc.scalar.activation(cTh[:, par, c], rawT[:, par, c], ACT.Copy).then_inc(s_hiT, 1)

            def hi_n(par, j):
                a, b = PAIR_TILES[j]
                nc.scalar.activation(cNh[:, par, a:b], rawN[:, par, a:b], ACT.Copy).then_inc(s_hiN, 1)

            def landed(sems, g, par):
                act.wait_ge(sems[par], (g - par) * 8 + 16)

            def exponentials(par, b):
                nc.scalar.activation(prob[:, b].rearrange("p (h k) -> p h k", h=2), psS[:, 2 * b:2 * b + 2, 0:HALF],
                                     ACT.Exp, bias=nb[:, par, b:b + 1], scale=SC,
                                     accum_out=rs[:, par, b:b + 1]).then_inc(s_exp, 1)

            def softmax(n, par):
                act.wait_ge(s_ref, 2 * n + 2)
                need(act, s_acc, 2 * n - 2)
                nc.scalar.activation(alpha[:, par, :], dm[:, par, :], ACT.Exp, scale=SC).then_inc(s_alpha, 1)
                need(act, s_T, PAIRS * n)
                for b in range(TB):
                    exponentials(par, b)

            def prob_hi(g, j):
                a, b = PAIR_TILES[j]
                act.wait_ge(s_T, PAIRS * g + j + 1)
                nc.scalar.activation(pTh[:, a:b], psT[:, j % 2, 0:(b - a) * TOK].rearrange("p (a t) -> p a t", t=TOK),
                                     ACT.Copy).then_inc(s_pth, 1)

            root(0)
            root(1)
            act.wait_ge(s_pe, 2)
            nc.scalar.activation(xnT[:, 2:4], cols(4)[:, 2:4], ACT.Copy).then_inc(s_eva, 1)
            act.wait_ge(s_small, 16 * 7)
            act.wait_ge(s_pe, 4)
            for c in (2, 3):
                last = nc.scalar.activation(qpT[:, c], cols(6)[:, c], ACT.Identity, bias=bq_sb[:, c:c + 1])
            last.then_inc(s_eva, 1)
            landed(s_rawT, 0, 0)
            for c in range(DC):
                hi_t(0, 0, c)
            for h in range(2):
                act.wait_ge(s_pe, 5 + h)
                nc.scalar.activation(qTh[:, 2 * h:2 * h + 2], cols(4)[:, 2 * h:2 * h + 2], ACT.Copy).then_inc(s_qh, 1)
            landed(s_rawT, 1, 1)
            for c in range(DC):
                hi_t(1, 1, c)
            landed(s_rawN, 0, 0)
            for j in range(PAIRS):
                hi_n(0, j)
            for b in range(TB):
                act.wait_ge(s_ref0, b + 1)
                exponentials(0, b)
            act.wait_ge(s_ref, 2)
            nc.scalar.activation(alpha[:, 0, :], dm[:, 0, :], ACT.Exp, scale=SC).then_inc(s_alpha, 1)

            def square_hi(m):
                if m < 2:
                    act.wait_ge(s_pe, 6)
                act.wait_ge(s_land, 16 * m + 16)
                nc.scalar.activation(square(m)[0], land[:], ACT.Copy, scale=WSC).then_inc(s_sqh, 1)

            def step(g, par, more_t=True, more=True):
                need(act, s_PV, 2 * g)
                for j in (0, 1):
                    prob_hi(g, j)
                if more_t:
                    landed(s_rawT, g + 2, par)
                    act.wait_ge(s_S, 2 * g + 2)
                    for c in range(DC):
                        hi_t(g + 2, par, c)
                for j in (2, 3):
                    prob_hi(g, j)
                if more:
                    landed(s_rawN, g + 1, 1 - par)
                    for j in (0, 1):
                        hi_n(1 - par, j)
                    softmax(g + 1, 1 - par)
                    for j in (2, 3):
                        hi_n(1 - par, j)

            step(0, 0)
            square_hi(0)
            for m in range(1, 4):
                step(2 * m - 1, 1)
                step(2 * m, 0)
                square_hi(m)
            with act.Fori(3, (NG - 4) // 2) as i:
                step(2 * i + 1, 1)
                step(2 * i + 2, 0)
            step(NG - 3, 1)
            step(NG - 2, 0, more_t=False)
            step(NG - 1, 1, more_t=False, more=False)

            def split_hi(e, par, k):
                act.wait_ge(s_wraw[k], 16 * e + 16)
                nc.scalar.activation(wh[:, par, k], landing[k], ACT.Copy, scale=WSC).then_inc(s_whi, 1)

            act.wait_ge(s_PV, 2 * NG)
            split_hi(0, 0, 0)
            for h in range(2):
                act.wait_ge(s_pe, 7 + h)
                nc.scalar.activation(t1h[:, 2 * h:2 * h + 2], cols(0)[:, 2 * h:2 * h + 2], ACT.Copy).then_inc(s_eva, 1)
            split_hi(0, 0, 1)
            split_hi(0, 0, 2)
            for c in range(DC):
                act.wait_ge(s_pe, 9 + c // 2)
                nc.scalar.activation(xph[:, c, TAPS - 1:], cols(2)[:, c], ACT.Identity, bias=bv_sb[:, c:c + 1],
                                     scale=1.0 / WSC).then_inc(s_zh, 1)
            split_hi(0, 0, 3)
            root(2)
            root(3)
            act.wait_ge(s_pe, 14)
            nc.scalar.activation(xph[:, 2:4, TAPS - 1:], cols(0)[:, 2:4], ACT.Copy).then_inc(s_xph, 1)
            nc.scalar.activation(xpad[:, 2:4, TAPS - 1:], cols(0)[:, 2:4], ACT.Copy).then_inc(s_x3, 1)
            act.wait_ge(s_ev, 7)
            nc.scalar.activation(xph[:, 0:2, TAPS - 1:], xpad[:, 0:2, TAPS - 1:], ACT.Copy).then_inc(s_xph, 1)
            for c in (0, 1):
                act.wait_ge(s_zero, 1 + 2 * (TAPS - 2) + c + 1)
                nc.scalar.activation(t1h[:, c], t1[:, c], ACT.Copy).then_inc(s_hth, 1)
            act.wait_ge(s_pe, 15)
            nc.scalar.activation(t1[:, 3], ps[:, 6, 0:TOK], ACT.Copy, scale=1.0 / WSC).then_inc(s_x3, 1)
            act.wait_ge(s_x3, 2)
            nc.scalar.activation(t1h[:, 3], t1[:, 3], ACT.Copy).then_inc(s_hth, 1)
            act.wait_ge(s_zero, H_DONE)
            nc.scalar.activation(t1h[:, 2], t1[:, 2], ACT.Copy).then_inc(s_hth, 1)
            root(4)
            root(5)
            for h in range(2):
                act.wait_ge(s_pe, 19 + h)
                nc.scalar.activation(xTh[:, 2 * h:2 * h + 2], cols(6)[:, 2 * h:2 * h + 2], ACT.Copy).then_inc(s_xh, 1)
            split_hi(0, 0, 4)
            split_hi(0, 0, 5)

            def silu(i, slot):
                act.wait_ge(s_H, i + 1)
                need(act, s_h, i - 1)
                nc.scalar.activation(sil[:, slot % 2], ps[:, slot, 0:TOK], ACT.Silu, scale=1.0 / WSC).then_inc(s_sil, 1)

            def hidden_hi(i, slot):
                act.wait_ge(s_h, i + 1)
                need(act, s_h2, i - 3)
                nc.scalar.activation(hh[:, slot], hf[:, slot % 2], ACT.Copy).then_inc(s_hh, 1)

            def gathered_rows(r, bank_h, bank_l):
                act.wait_ge(s_xg, r + 1)
                nc.scalar.activation(xgh[:], ps[:, bank_h, :].rearrange("p (c t) -> p c t", t=P), ACT.Copy)\
                    .then_inc(s_xgh, 1)
                nc.scalar.activation(xgl[:], ps[:, bank_l, :].rearrange("p (c t) -> p c t", t=P), ACT.Copy)\
                    .then_inc(s_xgl, 1)

            def expert(e, par):
                for b in range(HB):
                    i = HB * e + b
                    silu(i, b % 4)
                    if (e, b) == (0, 1):
                        act.wait_ge(s_gap, 1)
                        nc.scalar.activation(pr[:, :, 1:2], pr[:, :, 0:1], ACT.Exp).then_inc(s_gexp, 1)
                    if (e, b) == (0, 2):
                        nc.scalar.activation(xnh[:], acc[:], ACT.Copy).then_inc(s_xnh, 1)
                    if b == 2:
                        need(act, s_h2, HB * e)
                    if 2 <= b < HB - 1:
                        split_hi(e + 1, 1 - par, b - 2)
                    hidden_hi(i, b % 4)
                    if (e, b) == (ND - 1, HB - 2):
                        gathered_rows(0, 6, 7)
                    if b == HB - 1:
                        split_hi(e + 1, 1 - par, b - 2)

            for e in range(ND):
                expert(e, e % 2)

            def gathered(r):
                e, par = ND + r, (ND + r) % 2

                def half(h):
                    act.wait_ge(s_c1, 2 * r + h + 1)
                    need(act, s_cp, 2 * (r - 1) + h + 1)
                    nc.scalar.activation(csil[:, h], ps[:, 2 * h, :], ACT.Silu, scale=1.0 / WSC).then_inc(s_csil, 1)

                def hidden(h):
                    act.wait_ge(s_cT, 2 * r + h + 1)
                    nc.scalar.activation(chh[:, 4 * h:4 * h + 4], ps[:, 4 + h, :].rearrange("p (c t) -> p c t", t=P),
                                         ACT.Copy).then_inc(s_chh, 1)

                def split(k):
                    if r < NC - 1:
                        split_hi(e + 1, 1 - par, k)

                if r == 0:
                    act.wait_ge(s_h2, HB * ND)
                else:
                    act.wait_ge(s_cY, r)
                split(0)
                split(1)
                half(0)
                split(2)
                split(3)
                hidden(0)
                split(4)
                half(1)
                split(5)
                hidden(1)
                if r < NC - 1:
                    gathered_rows(r + 1, 4, 7)
                act.wait_ge(s_cY, r + 1)
                nc.scalar.activation(yh[:], ps[:, 6, :], ACT.Copy, scale=1.0 / WSC).then_inc(s_yh, 1)

            for r in range(NC):
                gathered(r)

        @block.vector
        def _(dve):
            V = nc.vector

            steps = [0]

            def done(ins):
                steps[0] += 1
                ins.then_inc(s_dve, 1)
                dve.wait_ge(s_dve, steps[0])

            def norm(m, src, dst, make):
                made = [0] * TB
                for b in range(TB):
                    if m == 0:
                        make(b)
                    else:
                        make(b).then_inc(s_dve, 1)
                        steps[0] += 1
                        made[b] = steps[0]
                    if b == 0:
                        need(dve, s_dve, made[0])
                        V.bn_stats(stats[:, 0], src[:, 0]).then_inc(s_stats, 1)
                dve.wait_ge(s_stats, m + 1)
                V.bn_aggr(mv[:, 0], stats[:, 0]).then_inc(s_mean, 1)
                need(dve, s_dve, made[1])
                V.bn_stats(stats[:, 1], src[:, 1]).then_inc(s_stats, 1)
                dve.wait_ge(s_mean, m + 1)
                V.tensor_scalar(var_e[:, 0:1], mv[:, 0, 1:2], EPS, None, ALU.add).then_inc(s_var, 1)
                dve.wait_ge(s_stats, m + 2)
                V.bn_aggr(mv[:, 1], stats[:, 1]).then_inc(s_mean, 1)
                dve.wait_ge(s_mean, m + 2)
                V.tensor_scalar(var_e[:, 1:2], mv[:, 1, 1:2], EPS, None, ALU.add).then_inc(s_var, 1)
                for b in range(TB):
                    dve.wait_ge(s_std, m + b + 1)
                    done(V.reciprocal(rstd[:, b:b + 1], std[:, b:b + 1]))
                    V.tensor_scalar(dst[:, b], src[:, b], mv[:, b, 0:1], rstd[:, b:b + 1],
                                    ALU.subtract, ALU.mult).then_inc(s_norm, 1)

            def lo_t(g, par, c):
                dve.wait_ge(s_hiT, 4 * g + c + 1)
                V.tensor_tensor(cTl[:, par, c], rawT[:, par, c], cTh[:, par, c], ALU.subtract).then_inc(s_loT, 1)

            def lo_n(g, par, j):
                a, b = PAIR_TILES[j]
                dve.wait_ge(s_hiN, 4 * g + j + 1)
                V.tensor_tensor(cNl[:, par, a:b], rawN[:, par, a:b], cNh[:, par, a:b], ALU.subtract).then_inc(s_loN, 1)

            def reference_max(n, par):
                for b in range(TB):
                    dve.wait_ge(s_S, 2 * n + b + 1)
                    V.tensor_reduce(cm[:, b:b + 1], psS[:, 2 * b:2 * b + 2, 0:HALF], AX.XY, ALU.max).then_inc(s_cm, 1)
                dve.wait_ge(s_cm, 2 * n + 2)
                V.tensor_tensor(mx[:, par], mx[:, 1 - par], cm[:], ALU.max).then_inc(s_mx, 1)
                dve.wait_ge(s_mx, n)
                V.tensor_scalar(nb[:, par], mx[:, par], -SC, LN_P, ALU.mult, ALU.add).then_inc(s_ref, 1)
                V.tensor_tensor(dm[:, par], mx[:, 1 - par], mx[:, par], ALU.subtract).then_inc(s_ref, 1)

            def prob_lo(g, j):
                a, b = PAIR_TILES[j]
                dve.wait_ge(s_pth, PAIRS * g + j + 1)
                V.tensor_tensor(pTl[:, a:b], psT[:, j % 2, 0:(b - a) * TOK].rearrange("p (a t) -> p a t", t=TOK),
                                pTh[:, a:b], ALU.subtract).then_inc(s_ptl, 1)

            def accumulate(g, par, final=False):
                dve.wait_ge(s_exp, 2 * g + 2)
                dve.wait_ge(s_alpha, g + 1)
                need(dve, s_den, 2 * g)
                for b in range(TB):
                    V.scalar_tensor_tensor(den[:, b:b + 1], den[:, b:b + 1], alpha[:, par, b:b + 1],
                                           rs[:, par, b:b + 1], ALU.mult, ALU.add).then_inc(s_den, 1)
                if final:
                    dve.wait_ge(s_den, 2 * NG)
                    done(V.reciprocal(rden[:], den[:]))
                need(dve, s_acc, 2 * g)
                for b in range(TB):
                    dve.wait_ge(s_PV, 2 * g + b + 1)
                    V.scalar_tensor_tensor(acc[:, b], acc[:, b], alpha[:, par, b:b + 1], psO[:, b],
                                           ALU.mult, ALU.add).then_inc(s_acc, 1)
                    if final:
                        dve.wait_ge(s_acc, 2 * g + b + 1)
                        V.tensor_scalar(acc[:, b], acc[:, b], rden[:, b:b + 1], None, ALU.mult).then_inc(s_ev, 1)

            V.memset(mx[:], -1e30).then_inc(s_init, 1)
            V.memset(den[:], 0.0).then_inc(s_init, 1)
            V.memset(acc[:], 0.0).then_inc(s_init, 1)
            norm(0, x_sb, xn, lambda b: dve.wait_ge(s_x[b], 16))
            dve.wait_ge(s_pe, 1)
            V.tensor_copy(xnT[:, 0:2], cols(4)[:, 0:2]).then_inc(s_ev, 1)
            dve.wait_ge(s_small, 16 * 7)
            dve.wait_ge(s_pe, 3)
            for c in (0, 1):
                last = V.tensor_scalar(qpT[:, c], cols(6)[:, c], bq_sb[:, c:c + 1], None, ALU.add)
            last.then_inc(s_ev, 1)
            for c in range(DC):
                lo_t(0, 0, c)
            for h in range(2):
                dve.wait_ge(s_qh, h + 1)
                V.tensor_tensor(qTl[:, 2 * h:2 * h + 2], cols(4)[:, 2 * h:2 * h + 2], qTh[:, 2 * h:2 * h + 2],
                                ALU.subtract).then_inc(s_ql, 1)
            for c in range(DC):
                lo_t(1, 1, c)
            dve.wait_ge(s_init, 3)
            for b in range(TB):
                dve.wait_ge(s_S, b + 1)
                V.tensor_reduce(cm[:, b:b + 1], psS[:, 2 * b:2 * b + 2, 0:HALF], AX.XY, ALU.max).then_inc(s_cm, 1)
                dve.wait_ge(s_cm, b + 1)
                done(V.tensor_tensor(mx[:, 0, b:b + 1], mx[:, 1, b:b + 1], cm[:, b:b + 1], ALU.max))
                V.tensor_scalar(nb[:, 0, b:b + 1], mx[:, 0, b:b + 1], -SC, LN_P, ALU.mult, ALU.add).then_inc(s_ref0, 1)
            V.tensor_tensor(dm[:, 0], mx[:, 1], mx[:, 0], ALU.subtract).then_inc(s_ref, 2)
            for j in range(PAIRS):
                lo_n(0, 0, j)

            def step(g, par, more_t=True, more=True):
                for j in (0, 1):
                    prob_lo(g, j)
                if more_t:
                    for c in (0, 1, 2):
                        lo_t(g + 2, par, c)
                for j in (2, 3):
                    prob_lo(g, j)
                if more_t:
                    lo_t(g + 2, par, 3)
                if more:
                    reference_max(g + 1, 1 - par)
                    for j in range(PAIRS):
                        lo_n(g + 1, 1 - par, j)
                accumulate(g, par, final=not more)

            def square_lo(m):
                dve.wait_ge(s_sqh, m + 1)
                hi, lo = square(m)
                V.scalar_tensor_tensor(lo.rearrange("p c n -> p (c n)"), land[:].rearrange("p c n -> p (c n)"), WSC,
                                       hi.rearrange("p c n -> p (c n)"), ALU.mult, ALU.subtract).then_inc(s_sql, 1)

            step(0, 0)
            square_lo(0)
            for m in range(1, 4):
                step(2 * m - 1, 1)
                step(2 * m, 0)
                square_lo(m)
            with dve.Fori(3, (NG - 4) // 2) as i:
                step(2 * i + 1, 1)
                step(2 * i + 2, 0)
            step(NG - 3, 1)
            step(NG - 2, 0, more_t=False)
            step(NG - 1, 1, more_t=False, more=False)

            def split_lo(e, par, k, a=0, b=PIECE):
                n = PIECES * e + k
                dve.wait_ge(s_whi, n + 1)
                last = V.scalar_tensor_tensor(wl[:, par, k, a:b], landing[k][:, a:b], WSC, wh[:, par, k, a:b],
                                              ALU.mult, ALU.subtract)
                if b == PIECE:
                    last.then_inc(s_wlo, 1)

            dve.wait_ge(s_PV, 2 * NG)
            V.memset(xpad[:, :, 0:TAPS - 1], 0.0)
            V.memset(xph[:, :, 0:TAPS - 1], 0.0)
            V.memset(xpl[:, :, 0:TAPS - 1], 0.0).then_inc(s_zero, 1)
            for h in range(2):
                dve.wait_ge(s_eva, 3 + h)
                V.tensor_tensor(t1l[:, 2 * h:2 * h + 2], cols(0)[:, 2 * h:2 * h + 2], t1h[:, 2 * h:2 * h + 2],
                                ALU.subtract).then_inc(s_ev, 1)
            for k in range(2):
                split_lo(0, 0, k)
            for c in range(DC):
                dve.wait_ge(s_zh, 2 * (c // 2) + 2)
                V.tensor_scalar(t2[:, c], cols(2)[:, c], 1.0 / WSC, bv_sb[:, c:c + 1], ALU.mult, ALU.add)\
                    .then_inc(s_x3d, 1)
                if c % 2 == 1:
                    dve.wait_ge(s_x3d, c + 1)
                    V.tensor_tensor(xpl[:, c - 1:c + 1, TAPS - 1:], t2[:, c - 1:c + 1], xph[:, c - 1:c + 1, TAPS - 1:],
                                    ALU.subtract).then_inc(s_zl, 1)
            split_lo(0, 0, 2)
            dve.wait_ge(s_res, TB)

            def attended(b):
                dve.wait_ge(s_pe, 11 + b)
                return V.scalar_tensor_tensor(x1[:, b], ps[:, 4 + b, :], 1.0 / WSC, x1[:, b], ALU.mult, ALU.add)

            norm(TB, x1, acc, attended)
            dve.wait_ge(s_pe, 13)
            V.tensor_copy(xpad[:, 0:2, TAPS - 1:], cols(0)[:, 0:2]).then_inc(s_ev, 1)
            dve.wait_ge(s_ev, 7)
            dve.wait_ge(s_x3, 1)
            dve.wait_ge(s_zero, 1)
            order_dve = [(c, j) for j in range(1, TAPS) for c in (0, 1)]
            order_dve += [(2, j) for j in range(1, TAPS) if (2, j) not in PE_TAPS]
            step_of = {}
            for n, (c, j) in enumerate(order_dve):
                src = xpad[:, c, TAPS - 1 - j:TAPS - 1 - j + TOK]
                tap = table_sb[:, c, j:j + 1]
                if j == 1:
                    last = V.tensor_scalar(t1[:, c], src, tap, None, ALU.mult)
                else:
                    dve.wait_ge(s_zero, step_of[c])
                    last = V.scalar_tensor_tensor(t1[:, c], src, tap, t1[:, c], ALU.mult, ALU.add)
                last.then_inc(s_zero, 1)
                step_of[c] = n + 2
            dve.wait_ge(s_pe, 16)
            dve.wait_ge(s_zero, step_of[2])
            V.scalar_tensor_tensor(t1[:, 2], ps[:, 7, 0:TOK], 1.0 / WSC, t1[:, 2], ALU.mult, ALU.add)\
                .then_inc(s_zero, 1)
            dve.wait_ge(s_hth, 4)
            V.tensor_tensor(t1l[:, 2], t1[:, 2], t1h[:, 2], ALU.subtract).then_inc(s_ht2, 1)
            dve.wait_ge(s_res, 2 * TB)

            def mixed(b):
                dve.wait_ge(s_pe, 17 + b)
                return V.scalar_tensor_tensor(macc[:, b], ps[:, 2 + b, :], 1.0 / WSC, x1[:, b], ALU.mult, ALU.add)

            norm(2 * TB, macc, acc, mixed)
            for h in range(2):
                dve.wait_ge(s_xh, h + 1)
                V.tensor_tensor(xTl[:, 2 * h:2 * h + 2], cols(6)[:, 2 * h:2 * h + 2], xTh[:, 2 * h:2 * h + 2],
                                ALU.subtract).then_inc(s_xl, 1)
            V.tensor_copy(t2[:], cols(6)).then_inc(s_ev, 1)
            dve.wait_ge(s_wlo, 4)
            split_lo(0, 0, 4)
            split_lo(0, 0, 5)

            def route_top():
                dve.wait_ge(s_pe, 21)
                for b in range(TB):
                    last = V.tensor_tensor(logits[:, b], ps[:, 6, NE * b:NE * b + NE], ebias_b[:], ALU.add)
                done(last)
                for b in range(TB):
                    last = V.max(top[:, b], logits[:, b])
                done(last)
                V.tensor_tensor(pr[:, :, 0:1], top[:, :, 1:2], top[:, :, 0:1], ALU.subtract).then_inc(s_gap, 1)
                for b in range(TB):
                    last = V.max_index(topi[:, b], top[:, b], logits[:, b])
                done(last)
                done(V.tensor_copy(topf[:], topi[:]))

            def route_weights():
                dve.wait_ge(s_gexp, 1)
                done(V.tensor_scalar(pr[:, :, 2:3], pr[:, :, 1:2], WSC * WSC, WSC * WSC, ALU.mult, ALU.add))
                done(V.reciprocal(pr[:, :, 2:3], pr[:, :, 2:3]))
                done(V.tensor_tensor(pr[:, :, 3:4], pr[:, :, 1:2], pr[:, :, 2:3], ALU.mult))
                dve.wait_ge(s_iota, 2)
                for b in range(TB):
                    for r in range(2):
                        last = V.tensor_scalar(sel[:, b, r], iota8[:], topf[:, b, r:r + 1], pr[:, b, 2 + r:3 + r],
                                               ALU.is_equal, ALU.mult)
                    last = V.tensor_scalar(second16[:, b], iota8[:], topf[:, b, 1:2], None, ALU.is_equal)
                done(last)
                for b in range(TB):
                    last = V.scalar_tensor_tensor(chosen16[:, b], iota8[:], topf[:, b, 0:1], second16[:, b],
                                                  ALU.is_equal, ALU.add)
                last.then_inc(s_chosen, 1)
                done(V.tensor_tensor(cbase[:], sel[:, :, 0], sel[:, :, 1], ALU.add))

            def route_order():
                dve.wait_ge(s_load, 1)
                done(V.tensor_copy(load[:], ps[:, 6, 0:NE]))
                done(V.max(load_top[:], load[:]))
                V.max_index(order[:], load_top[:], load[:]).then_inc(s_order, 1)
                dve.wait_ge(s_order, 1)
                done(V.tensor_copy(order_f[:], order[:]))
                for b in range(TB):
                    for r in range(NE):
                        last = V.scalar_tensor_tensor(picked[:, b, r], iota8[:], order_f[:, r:r + 1], cbase[:, b],
                                                      ALU.is_equal, ALU.mult, accum_out=comb[:, b, NS + r:NS + r + 1])
                done(last)

            def route_mine():
                V.tensor_scalar(mine16[:], comb[:, :, ND:NX], 0.0, None, ALU.is_gt).then_inc(s_mine, 1)
                V.tensor_scalar(mine[:], comb[:, :, ND:NX], 0.0, None, ALU.is_gt).then_inc(s_mine, 1)
                dve.wait_ge(s_mine, 2)
                done(V.tensor_scalar(comb[:, :, ND:NX], comb[:, :, ND:NX], WSC, None, ALU.mult))

            def route_places():
                dve.wait_ge(s_slot, 1)
                done(V.tensor_copy(slot[:], ps[:, 6, 0:TB * NC].rearrange("p (b r) -> p b r", r=NC)))
                dve.wait_ge(s_iota, 3)
                for r in range(NC):
                    for b in range(TB):
                        last = V.tensor_scalar(place[:, r, b], iota_s[:], slot[:, b, r:r + 1], mine[:, b, r:r + 1],
                                               ALU.is_equal, ALU.mult)
                last.then_inc(s_place, 1)

            def route_places_t():
                dve.wait_ge(s_placeT, 1)
                V.tensor_copy(placeT[:, 0:4], ps[:, 6, :].bitcast(F16).rearrange("p (r t) -> p r t", t=TOK))\
                    .then_inc(s_placed, 1)
                V.tensor_copy(placeT[:, 4], ps[:, 7, 0:TOK // 2].bitcast(F16)).then_inc(s_placed, 1)

            def rows_lo():
                dve.wait_ge(s_xnh, 1)
                V.tensor_tensor(xnl[:], acc[:], xnh[:], ALU.subtract).then_inc(s_xnl, 1)

            routing = {(0, 1): route_top, (0, 2): route_weights, (0, 3): rows_lo, (0, 6): route_order,
                       (0, 7): route_mine, (1, 4): route_places, (2, 4): route_places_t}

            def product(i, slot):
                dve.wait_ge(s_sil, i + 1)
                need(dve, s_hl, i - 1)
                V.tensor_tensor(hf[:, slot % 2], sil[:, slot % 2], ps[:, slot, TOK:2 * TOK], ALU.mult)\
                    .then_inc(s_h, 1)

            def hidden_lo(i, slot):
                dve.wait_ge(s_hh, i + 1)
                V.tensor_tensor(hl[:, slot], hf[:, slot % 2], hh[:, slot], ALU.subtract).then_inc(s_hl, 1)

            def combine(e):
                for b in range(TB):
                    if e >= ND:
                        dve.wait_ge(s_cs, TB * (e - ND) + b + 1)
                        bank = 7 - b
                    elif b == 0:
                        dve.wait_ge(s_Y, e + 1)
                        bank = 4
                    else:
                        dve.wait_ge(s_h2, HB * e + HB)
                        bank = 5
                    need(dve, s_macc, TB * e)
                    V.scalar_tensor_tensor(macc[:, b], ps[:, bank, :], comb[:, b, e:e + 1], macc[:, b],
                                           ALU.mult, ALU.add).then_inc(s_macc, 1)

            def expert(e, par):
                for b in range(HB):
                    i = HB * e + b
                    if e > 0 and b == 2:
                        combine(e - 1)
                    product(i, b % 4)
                    if (e, b) in routing:
                        routing[e, b]()
                    if 2 <= b < HB - 1:
                        split_lo(e + 1, 1 - par, b - 2)
                    hidden_lo(i, b % 4)
                    if b == HB - 1:
                        split_lo(e + 1, 1 - par, b - 2)

            for e in range(ND):
                expert(e, e % 2)

            def gathered(r):
                e, par = ND + r, (ND + r) % 2

                def half(h):
                    dve.wait_ge(s_csil, 2 * r + h + 1)
                    need(dve, s_cT, 2 * (r - 1) + h + 1)
                    V.tensor_tensor(ch[:, h], csil[:, h], ps[:, 2 * h + 1, :], ALU.mult).then_inc(s_cp, 1)

                def hidden(h):
                    dve.wait_ge(s_chh, 2 * r + h + 1)
                    V.tensor_tensor(chl[:, 4 * h:4 * h + 4], ps[:, 4 + h, :].rearrange("p (c t) -> p c t", t=P),
                                    chh[:, 4 * h:4 * h + 4], ALU.subtract).then_inc(s_chl, 1)

                def split(k, a=0, b=PIECE):
                    if r < NC - 1:
                        split_lo(e + 1, 1 - par, k, a, b)

                if r == 0:
                    combine(ND - 1)
                split(0)
                split(1)
                half(0)
                if r > 0:
                    combine(e - 1)
                split(2)
                hidden(0)
                split(3, 0, PIECE // 2)
                half(1)
                split(3, PIECE // 2)
                hidden(1)
                split(4)
                split(5)
                dve.wait_ge(s_yh, r + 1)
                V.scalar_tensor_tensor(yl[:], ps[:, 6, :], 1.0 / WSC, yh[:], ALU.mult, ALU.subtract).then_inc(s_yl, 1)

            for r in range(NC):
                gathered(r)
            combine(NX - 1)

        @block.tensor
        def _(pe):
            mm = nc.tensor.matmul

            def transpose_rows(bank, src, sem, count):
                for b in range(TB):
                    pe.wait_ge(sem, count + b + 1)
                    for c in range(DC):
                        last = nc.tensor.transpose(cols(bank)[:, c, b * P:(b + 1) * P], src[:, b, c * P:(c + 1) * P],
                                                   ident[:])
                        if b == TB - 1 and c % 2 == 1:
                            last.then_inc(s_pe, 1)

            def project_t(bank, w, src):
                for o, cs in ((0, (0, 1)), (2, (0, 1)), (0, (2, 3)), (1, range(DC)), (2, (2, 3)), (3, range(DC))):
                    for c in cs:
                        if o == 0 and c % 2 == 0:
                            pe.wait_ge(s_ev if c == 0 else s_eva, w + 1)
                        last = mm(cols(bank)[:, o], wts[:, w, c, o * P:(o + 1) * P], src[:, c],
                                  start=(c == 0), stop=(c == DC - 1))
                    if o % 2 == 1:
                        last.then_inc(s_pe, 1)

            def scores(n, par, b, first=False):
                for q, k in ((qTh, cTh), (qTh, cTl), (qTl, cTh)):
                    for c in range(DC):
                        if first and k is cTh and c % 2 == 0:
                            pe.wait_ge(s_qh if q is qTh else s_ql, c // 2 + 1)
                        for h in range(2):
                            last = mm(psS[:, 2 * b + h, 0:HALF], q[:, c, b * P:(b + 1) * P],
                                      k[:, par, c, h * HALF:(h + 1) * HALF],
                                      start=(c == 0 and q is qTh and k is cTh), stop=(c == DC - 1 and q is qTl))
                last.then_inc(s_S, 1)

            def transposes(g, j):
                a, b = PAIR_TILES[j]
                for t in range(a, b):
                    for q in range(TB):
                        last = nc.tensor.transpose(psT[:, j % 2, (t - a) * TOK + q * P:(t - a) * TOK + (q + 1) * P],
                                                   prob[:, q, t * P:(t + 1) * P], ident[:])
                last.then_inc(s_T, 1)

            def keep_warm(count, bank):
                for _ in range(count):
                    mm(ps[:, bank, 0:P], ident[:], ident[:], start=True, stop=True)

            pe.wait_ge(s_ident, 2)
            keep_warm(11, 0)
            transpose_rows(4, xn, s_norm, 0)
            pe.wait_ge(s_wq, 16)
            project_t(6, 0, xnT)
            pe.wait_ge(s_wk, 16)
            project_t(4, 1, qpT)
            pe.wait_ge(s_hiT, 4)
            pe.wait_ge(s_loT, 4)
            for b in range(TB):
                scores(0, 0, b, first=(b == 0))
            keep_warm(8, 4)

            def step(g, par, more=True):
                pe.wait_ge(s_exp, 2 * g + 2)
                need(pe, s_ptl, PAIRS * g)
                for j in (0, 1):
                    transposes(g, j)
                if more:
                    pe.wait_ge(s_hiT, 4 * g + 8)
                    pe.wait_ge(s_loT, 4 * g + 8)
                    scores(g + 1, 1 - par, 0)
                for j in (2, 3):
                    pe.wait_ge(s_ptl, PAIRS * g + j - 1)
                    transposes(g, j)
                if more:
                    scores(g + 1, 1 - par, 1)
                pe.wait_ge(s_hiN, 4 * g + 4)
                pe.wait_ge(s_loN, 4 * g + 4)
                need(pe, s_acc, 2 * g)
                for b in range(TB):
                    for t in range(KT):
                        if b == 0 and t % 2 == 0:
                            pe.wait_ge(s_pth, PAIRS * g + t // 2 + 1)
                            pe.wait_ge(s_ptl, PAIRS * g + t // 2 + 1)
                        for p, k in ((pTh, cNh), (pTh, cNl), (pTl, cNh)):
                            last = mm(psO[:, b, :], p[:, t, b * P:(b + 1) * P], k[:, par, t],
                                      start=(t == 0 and p is pTh and k is cNh), stop=(t == KT - 1 and p is pTl))
                    last.then_inc(s_PV, 1)

            step(0, 0)
            with pe.Fori(0, (NG - 4) // 2) as i:
                step(2 * i + 1, 1)
                step(2 * i + 2, 0)
            step(NG - 3, 1)
            step(NG - 2, 0)
            step(NG - 1, 1, more=False)

            transpose_rows(0, acc, s_ev, 2)

            def parts(out, lhs, rhs, first, final):
                mm(out, lhs[0], rhs[0], start=first, stop=False)
                mm(out, lhs[0], rhs[1], start=False, stop=False)
                return mm(out, lhs[1], rhs[0], start=False, stop=final)

            pe.wait_ge(s_sql, 4)
            sq = [square(m) for m in range(4)]
            for o in range(DC):
                for w, x16 in ((0, t1h), (1, t1h), (0, t1l)):
                    for c in range(DC):
                        if o == 0 and w == 0 and c % 2 == 0:
                            if x16 is t1h:
                                pe.wait_ge(s_eva, 3 + c // 2)
                            else:
                                pe.wait_ge(s_ev, 5 + c // 2)
                        last = mm(cols(2)[:, o], sq[0][w][:, c, o * P:(o + 1) * P], x16[:, c],
                                  start=(c == 0 and w == 0 and x16 is t1h), stop=(c == DC - 1 and x16 is t1l))
                if o % 2 == 1:
                    last.then_inc(s_pe, 1)

            def rows(pair, c, b, pad=0):
                return [t[:, c, pad + b * P:pad + (b + 1) * P] for t in pair]

            def of(m, c):
                return [w[:, c] for w in sq[m]]

            def hi_rows(bank, b, pair, m, c, pad, first):
                for p in range(2):
                    mm(ps[:, bank, :], rows(pair, c, b, pad)[0], of(m, c)[p], start=(first and p == 0), stop=False)

            def lo_rows(bank, b, pair, m, c, pad, final):
                return mm(ps[:, bank, :], rows(pair, c, b, pad)[1], of(m, c)[0], start=False, stop=final)

            for c in range(DC):
                pe.wait_ge(s_zh, c + 1)
                hi_rows(4, 0, (xph, xpl), 1, c, TAPS - 1, c == 0)
            for c in range(2):
                hi_rows(5, 1, (xph, xpl), 1, c, TAPS - 1, c == 0)
            for c in range(DC):
                pe.wait_ge(s_zl, c // 2 + 1)
                last = lo_rows(4, 0, (xph, xpl), 1, c, TAPS - 1, c == DC - 1)
            last.then_inc(s_pe, 1)
            for c in range(2, DC):
                hi_rows(5, 1, (xph, xpl), 1, c, TAPS - 1, False)
            for c in range(DC):
                last = lo_rows(5, 1, (xph, xpl), 1, c, TAPS - 1, c == DC - 1)
            last.then_inc(s_pe, 1)
            keep_warm(8, 7)
            transpose_rows(0, acc, s_norm, TB)
            for n, cs in enumerate(((2, 3), (0, 1))):
                pe.wait_ge(s_xph, n + 1)
                for b in range(TB):
                    for c in cs:
                        for p in range(2):
                            mm(ps[:, 2 + b, :], rows((xph, xpl), c, b, TAPS - 1)[0], of(2, c)[p],
                               start=(c == 2 and p == 0), stop=False)
            pe.wait_ge(s_xpl, 2)
            for b in range(TB):
                for c in range(DC):
                    mm(ps[:, 2 + b, :], rows((xph, xpl), c, b, TAPS - 1)[1], of(2, c)[0], start=False, stop=False)
            pe.wait_ge(s_diag, 3 * len(PE_TAPS))
            pe.wait_ge(s_zero, 1)
            for n, (c, j) in enumerate(PE_TAPS):
                final = n + 1 == len(PE_TAPS) or PE_TAPS[n + 1][0] != c
                last = parts(ps[:, 6 if c == 3 else 7, 0:TOK], (diagh[:, n], diagl[:, n]),
                             [t[:, c, TAPS - 1 - j:TAPS - 1 - j + TOK] for t in (xph, xpl)],
                             n == 0 or PE_TAPS[n - 1][0] != c, final)
                if final:
                    last.then_inc(s_pe, 1)
            def chunk(b, c):
                if c < 2:
                    pe.wait_ge(s_hth, c + 1)
                    pe.wait_ge(s_htl, c + 1)
                elif c == 3:
                    pe.wait_ge(s_hth, 3)
                    pe.wait_ge(s_htl, 3)
                else:
                    pe.wait_ge(s_hth, 4)
                    pe.wait_ge(s_ht2, 1)
                return parts(ps[:, 2 + b, :], rows((t1h, t1l), c, b), of(3, c), False, c == 2)

            for b, c in ((0, 0), (0, 1), (0, 3), (1, 0), (1, 1)):
                chunk(b, c)
            chunk(0, 2).then_inc(s_pe, 1)
            chunk(1, 3)
            chunk(1, 2).then_inc(s_pe, 1)
            keep_warm(6, 5)
            transpose_rows(6, acc, s_norm, 2 * TB)

            def router_logits():
                pe.wait_ge(s_ev, 8)
                for b in range(TB):
                    for c in range(DC):
                        last = mm(ps[:, 6, NE * b:NE * b + NE], t2[:, c, b * P:(b + 1) * P], router_sb[:, c],
                                  start=(c == 0), stop=(c == DC - 1))
                last.then_inc(s_pe, 1)

            def first(e, par, b):
                i = HB * e + b
                if b == 0:
                    pe.wait_ge(s_whi, PIECES * e + 4)
                    pe.wait_ge(s_wlo, PIECES * e + 4)
                need(pe, s_h, i - 3)
                for m in range(2):
                    for w, xt in ((wh, xTh), (wl, xTh), (wh, xTl)):
                        for c in range(DC):
                            if i == 0 and m == 0 and w is wh and c % 2 == 0:
                                pe.wait_ge(s_xh if xt is xTh else s_xl, c // 2 + 1)
                            last = mm(ps[:, b % 4, m * TOK:(m + 1) * TOK], w13(w, par, m)[:, c, b * P:(b + 1) * P],
                                      xt[:, c], start=(c == 0 and w is wh and xt is xTh),
                                      stop=(c == DC - 1 and xt is xTl))
                last.then_inc(s_H, 1)

            def second(e, par, b):
                i = HB * e + b
                if b == 0:
                    pe.wait_ge(s_whi, PIECES * e + PIECES)
                    pe.wait_ge(s_wlo, PIECES * e + PIECES)
                    need(pe, s_macc, TB * e)
                pe.wait_ge(s_hh, i + 1)
                pe.wait_ge(s_hl, i + 1)
                for q in range(TB):
                    for h, w in ((hh, wh), (hh, wl), (hl, wh)):
                        last = mm(ps[:, 4 + q, :], h[:, b % 4, q * P:(q + 1) * P], w2(w, par)[:, b],
                                  start=(b == 0 and h is hh and w is wh), stop=(b == HB - 1 and h is hl))
                    if b == HB - 1 and q == 0:
                        last.then_inc(s_Y, 1)
                last.then_inc(s_h2, 1)

            def count_rows():
                pe.wait_ge(s_chosen, 1)
                pe.wait_ge(s_iota, 6)
                for b in range(TB):
                    last = mm(ps[:, 6, 0:NE], ones16[:], chosen16[:, b], start=(b == 0), stop=(b == TB - 1))
                last.then_inc(s_load, 1)

            def number_rows():
                pe.wait_ge(s_mine, 1)
                mm(ps[:, 6, 0:NC], before16[:], mine16[:, 0], start=True, stop=True)
                mm(ps[:, 6, NC:2 * NC], ones16[:], mine16[:, 0], start=True, stop=False)
                mm(ps[:, 6, NC:2 * NC], before16[:], mine16[:, 1], start=False, stop=True).then_inc(s_slot, 1)

            def turn_places():
                pe.wait_ge(s_place, 1)
                for r in range(NC):
                    for b in range(TB):
                        o = ((r % 4) * TB + b) * P
                        last = nc.tensor.transpose(ps[:, 6 + r // 4, :].bitcast(F16)[:, o:o + P], place[:, r, b],
                                                   ident16[:])
                last.then_inc(s_placeT, 1)

            def gather(r, bank_h, bank_l):
                for bank, rows in ((bank_h, xnh), (bank_l, xnl)):
                    for c in range(DC):
                        for b in range(TB):
                            last = mm(ps[:, bank, c * P:(c + 1) * P], rows[:, b, c * P:(c + 1) * P], place[:, r, b],
                                      start=(b == 0), stop=(b == TB - 1))
                last.then_inc(s_xg, 1)

            def first_gather():
                pe.wait_ge(s_xnl, 1)
                pe.wait_ge(s_placed, 2)
                gather(0, 6, 7)

            routing = {(0, 4): count_rows, (1, 2): number_rows, (2, 2): turn_places, (ND - 1, 5): first_gather}

            def expert(e, par):
                for b in range(2, HB + 2):
                    if b < HB:
                        first(e, par, b)
                    elif e < ND - 1:
                        first(e + 1, 1 - par, b - HB)
                    if (e, b) in routing:
                        routing[e, b]()
                    second(e, par, b - 2)

            def scatter(r):
                pe.wait_ge(s_yh, r + 1)
                for b in range(TB):
                    mm(ps[:, 7 - b, :], placeT[:, r, b * P:(b + 1) * P], yh[:], start=True, stop=False)
                    if b == 0:
                        pe.wait_ge(s_yl, r + 1)
                    mm(ps[:, 7 - b, :], placeT[:, r, b * P:(b + 1) * P], yl[:], start=False, stop=True)\
                        .then_inc(s_cs, 1)

            def gathered(r):
                e, par = ND + r, (ND + r) % 2

                def matrix(m, h):
                    for w, xt in ((wh, xgh), (wl, xgh), (wh, xgl)):
                        if xt is xgl:
                            pe.wait_ge(s_xgl, r + 1)
                        for c in range(DC):
                            last = mm(ps[:, 2 * h + m, :], xt[:, c], w13(w, par, m)[:, c, h * HH:(h + 1) * HH],
                                      start=(c == 0 and w is wh and xt is xgh), stop=(c == DC - 1 and xt is xgl))
                    return last

                def turn(h):
                    pe.wait_ge(s_cp, 2 * r + h + 1)
                    for c in range(4):
                        last = nc.tensor.transpose(ps[:, 4 + h, c * P:(c + 1) * P], ch[:, h, c * P:(c + 1) * P],
                                                   ident[:])
                    last.then_inc(s_cT, 1)

                def output(h):
                    pe.wait_ge(s_chh, 2 * r + h + 1)
                    for hd, w in ((chh, wh), (chh, wl), (chl, wh)):
                        if hd is chl:
                            pe.wait_ge(s_chl, 2 * r + h + 1)
                        for b in range(4 * h, 4 * h + 4):
                            last = mm(ps[:, 6, :], hd[:, b], w2(w, par)[:, b],
                                      start=(b == 0 and hd is chh and w is wh), stop=(b == HB - 1 and hd is chl))
                    return last

                pe.wait_ge(s_xgh, r + 1)
                pe.wait_ge(s_whi, PIECES * e + 4)
                pe.wait_ge(s_wlo, PIECES * e + 4)
                need(pe, s_cp, 2 * r - 1)
                if r == 0:
                    pe.wait_ge(s_h, HB * ND)
                matrix(0, 0)
                matrix(1, 0).then_inc(s_c1, 1)
                if r > 0:
                    scatter(r - 1)
                    pe.wait_ge(s_cp, 2 * r)
                matrix(0, 1)
                if r == 0:
                    pe.wait_ge(s_macc, TB * ND)
                turn(0)
                matrix(1, 1).then_inc(s_c1, 1)
                pe.wait_ge(s_whi, PIECES * e + PIECES)
                pe.wait_ge(s_wlo, PIECES * e + PIECES)
                pe.wait_ge(s_macc, TB * e)
                output(0)
                turn(1)
                if r < NC - 1:
                    gather(r + 1, 4, 7)
                output(1).then_inc(s_cY, 1)

            first(0, 0, 0)
            router_logits()
            first(0, 0, 1)
            for e in range(ND):
                expert(e, e % 2)
            for r in range(NC):
                gathered(r)
            scatter(NC - 1)


def kernel(**inputs):
    import numpy as np
    import concourse.bacc as bacc
    from concourse.bass_utils import run_bass_kernel_spmd

    a = {name: np.asarray(v) for name, v in inputs.items()}

    def chunks(w):
        return w.reshape(DC, P, -1).transpose(1, 0, 2)

    def piece(w):
        return w.reshape(-1, P, w.shape[1]).transpose(1, 0, 2).reshape(P, -1)

    f = "L0_ffn_"
    experts = [(a[f + "sw1"][i], a[f + "sw3"][i], a[f + "sw2"][i]) for i in range(NS)]
    experts += [(a[f + "w1"][i], a[f + "w3"][i], a[f + "w2"][i]) for i in range(NE)]
    ctx = a["ctx_1024"].reshape(NG, P, KT, DC, P)
    arrays = {
        "x": a["x"],
        "ctx_nat": ctx.reshape(NG, P, KT, D),
        "ctx_t": ctx.transpose(0, 4, 3, 2, 1).reshape(NG, P, DC, GK),
        "wmats": np.stack([chunks(a["L0_xattn_Wq"].T), chunks(a["L0_xattn_Wk"]), chunks(a["L0_xattn_Wv"].T),
                           chunks(a["L0_xattn_Wo"].T), chunks(a["L0_attn_W1"]), chunks(a["L0_attn_W2"])]),
        "bq": a["L0_xattn_bq"].reshape(DC, P).T,
        "bv": a["L0_xattn_bv"].reshape(DC, P).T,
        "bo": a["L0_xattn_bo"],
        "bias": a["L0_attn_bias"],
        "table": chunks(a["L0_attn_embeddings_table"].T),
        "router": chunks(a[f + "router_w"].T),
        "ebias": a[f + "expert_bias"],
        "wexp": np.stack([np.concatenate([piece(w1.T), piece(w3.T), piece(w2.T)], axis=1) for w1, w3, w2 in experts]),
    }
    nc = bacc.Bacc("TRN2", target_bir_lowering=False, num_devices=1)
    args, ins = [], {}
    for name, v in arrays.items():
        ins[f"{name}_dram"] = np.ascontiguousarray(v)
        args.append(nc.dram_tensor(f"{name}_dram", v.shape, mybir.dt.from_np(v.dtype), kind="ExternalInput").ap())
    args.append(nc.dram_tensor("out_dram", a["x"].shape, F32, kind="ExternalOutput").ap())
    perceiver_kernel(nc, *args)
    r = run_bass_kernel_spmd(nc, [ins], core_ids=[0])
    return r.results[0]["out_dram"]
```
